# Optimizing a Trainium2 kernel written in Bass

```python
import numpy as np
import jax
import jax.numpy as jnp

def _softmax(x, axis=-1):
    return jax.nn.softmax(x, axis=axis)

def _gelu(x):
    return jax.nn.gelu(x, approximate=True)

def _silu(x):
    return jax.nn.silu(x)

def _sigmoid(x):
    return jax.nn.sigmoid(x)

def _layernorm(x, axis=-1, eps=1e-05):
    m = jnp.mean(x, axis=axis, keepdims=True)
    v = jnp.var(x, axis=axis, keepdims=True)
    return (x - m) / jnp.sqrt(v + eps)

def _scatter_add(tgt, idx, src, axis=0):
    return tgt.at[idx].add(src)

def _segment_sum(src, seg, n):
    return jax.ops.segment_sum(src, seg, n)
kernel_name = 'mk_adj_preln_d1_adj_r2_0f634a'

def setup_inputs(seed: int=0):
    np.random.seed(seed)
    _w = jnp.asarray

    def _rec_inputs():
        import jax
        import jax.numpy as jnp
        _gk = jax.random.key(seed)
        x = -0.0005207 + 1.001 * jax.random.normal(jax.random.fold_in(_gk, 1), (4096, 128), jnp.float32)
        _w = (1.0 + jnp.arange(4096, dtype=jnp.float32)) ** (-0.5)
        _w = _w / _w.mean()
        _pij = jnp.clip(0.000488281 * _w[:, None] * _w[None, :], 0.0, 1.0)
        _a = jax.random.uniform(jax.random.fold_in(_gk, 2), (4096, 4096)) < _pij
        adj = _a.astype(jnp.int32)
        return (x, adj)
    x, adj = _rec_inputs()

    def _L0_gnn_setup():
        import jax, jax.numpy as jnp
        import numpy as np
        MIN_NORM = 1e-15
        EPS = 1e-07
        MASK_FILL = -9000000000000000.0

        def logmap0(x, c):
            K = 1.0 / c
            sqrtK = K ** 0.5
            y = x[:, 1:]
            y_norm = jnp.clip(jnp.linalg.norm(y, axis=-1, keepdims=True), MIN_NORM)
            theta = jnp.clip(x[:, :1] / sqrtK, 1.0 + EPS)
            res = sqrtK * jnp.arccosh(theta) * y / y_norm
            return jnp.concatenate([jnp.zeros_like(x[:, :1]), res], axis=1)

        def proj(x, c):
            K = 1.0 / c
            y = x[:, 1:]
            x0 = jnp.sqrt(K + jnp.sum(y * y, axis=-1, keepdims=True))
            return jnp.concatenate([x0, y], axis=1)

        def expmap0(u, c):
            K = 1.0 / c
            sqrtK = K ** 0.5
            x = u[:, 1:]
            x_norm = jnp.clip(jnp.linalg.norm(x, axis=-1, keepdims=True), MIN_NORM)
            theta = x_norm / sqrtK
            res = jnp.concatenate([sqrtK * jnp.cosh(theta), sqrtK * jnp.sinh(theta) * x / x_norm], axis=1)
            return proj(res, c)
        key = jax.random.key(seed)
        k1, k2, k3, k4, k5 = jax.random.split(key, 5)
        N, D_in, D_out = (4096, 128, 128)
        x = jax.random.normal(k1, (N, D_in), dtype=jnp.float32)
        adj = jax.random.randint(k2, (N, N), 0, 2, dtype=jnp.int32)
        W_gcn = jax.random.normal(k3, (D_in - 1, D_out - 1), dtype=jnp.float32)
        std_w = 1.414 * (2.0 / (D_out + D_out)) ** 0.5
        W_att = jax.random.normal(k4, (D_out, D_out), dtype=jnp.float32) * std_w
        std_a = 1.414 * (2.0 / (2 * D_out + 1)) ** 0.5
        a_att = jax.random.normal(k5, (2 * D_out, 1), dtype=jnp.float32) * std_a
        return {'x': x, 'adj': adj, 'k': 1, 'W_gcn': W_gcn, 'W_att': W_att, 'a_att': a_att}
    _L0_gnn_all = _L0_gnn_setup()
    _L0_gnn_in = {k: v for k, v in _L0_gnn_all.items() if k in ('W_gcn', 'W_att', 'a_att')}
    del _L0_gnn_all
    return {'x': x, 'adj': adj, 'L0_gnn_W_gcn': _L0_gnn_in['W_gcn'], 'L0_gnn_W_att': _L0_gnn_in['W_att'], 'L0_gnn_a_att': _L0_gnn_in['a_att']}

def reference(x, adj, L0_gnn_W_gcn, L0_gnn_W_att, L0_gnn_a_att):
    import jax
    import jax.numpy as jnp

    def _L0_gnn_ref(x, adj, k, W_gcn, W_att, a_att):
        import jax, jax.numpy as jnp
        import numpy as np
        MIN_NORM = 1e-15
        EPS = 1e-07
        MASK_FILL = -9000000000000000.0

        def logmap0(x, c):
            K = 1.0 / c
            sqrtK = K ** 0.5
            y = x[:, 1:]
            y_norm = jnp.clip(jnp.linalg.norm(y, axis=-1, keepdims=True), MIN_NORM)
            theta = jnp.clip(x[:, :1] / sqrtK, 1.0 + EPS)
            res = sqrtK * jnp.arccosh(theta) * y / y_norm
            return jnp.concatenate([jnp.zeros_like(x[:, :1]), res], axis=1)

        def proj(x, c):
            K = 1.0 / c
            y = x[:, 1:]
            x0 = jnp.sqrt(K + jnp.sum(y * y, axis=-1, keepdims=True))
            return jnp.concatenate([x0, y], axis=1)

        def expmap0(u, c):
            K = 1.0 / c
            sqrtK = K ** 0.5
            x = u[:, 1:]
            x_norm = jnp.clip(jnp.linalg.norm(x, axis=-1, keepdims=True), MIN_NORM)
            theta = x_norm / sqrtK
            res = jnp.concatenate([sqrtK * jnp.cosh(theta), sqrtK * jnp.sinh(theta) * x / x_norm], axis=1)
            return proj(res, c)
        c = float(k)
        N = x.shape[0]
        logx = logmap0(x, c)
        Wx = logx[:, 1:] @ W_gcn
        tmp = jnp.concatenate([jnp.zeros((N, 1), x.dtype), Wx], axis=1)
        fun7 = proj(expmap0(tmp, c), c)
        h_in = logmap0(fun7, c)
        h = h_in @ W_att
        F_ = h.shape[1]
        e = h @ a_att[:F_] + (h @ a_att[F_:]).T
        att = jnp.where(adj > 0, e, MASK_FILL)
        att = jax.nn.softmax(att, axis=1)
        h_prime = att @ h
        emb = jax.nn.elu(h_prime)
        emb = proj(emb, c)
        out = expmap0(jax.nn.sigmoid(logmap0(emb, c)), c)
        return out
    h = jnp.maximum(_layernorm(x, axis=-1), 0.0)
    x = x + _L0_gnn_ref(h, adj, 1, L0_gnn_W_gcn, L0_gnn_W_att, L0_gnn_a_att)
    return x

_drawn_inputs = setup_inputs


def setup_inputs(seed=0):
    import zlib

    import numpy as np

    out = dict(_drawn_inputs(seed))
    spreads = {}
    factors = {}
    for name, (base, spread) in spreads.items():
        noise = np.random.default_rng([zlib.crc32(name.encode()), seed]).standard_normal(out[name].shape)
        drawn = base * np.exp(spread * noise) if base else spread * noise
        out[name] = jnp.asarray(drawn.astype(out[name].dtype))
    for name, factor in factors.items():
        out[name] = (out[name] * factor).astype(out[name].dtype)
    return out
```

```python
import concourse.bass as bass
from concourse import mybir
from contextlib import ExitStack

P = 128
N = 4096
F = 128
TILES = N // P
GT = 4
GROUPS = TILES // GT
GW = GT * P
CHUNKS = 4
CT = TILES // CHUNKS
SLOTS = 2 * CHUNKS
QUARTERS = 4
QT = TILES // QUARTERS
EPS = 2.0 ** -23
ROOT_EPS = (EPS * (EPS + 2.0)) ** 0.5
G_SCALE = 512.0
RSQRT_SEED = 0x5F3759DF


class Chain:

    def __init__(self, eng, sem):
        self.eng, self.sem, self.base, self.n = eng, sem, 0, 0

    def __call__(self, ins):
        self.n += 1
        ins.then_inc(self.sem, 1)
        self.eng.wait_ge(self.sem, self.base + self.n)

    def enter(self, it, per):
        self.before, self.per = self.n, per
        self.base, self.n = it * per + self.before, 0

    def leave(self, trips):
        assert self.n == self.per, self.n
        self.base, self.n = 0, self.before + trips * self.per


def layer(nc, x, adj, wg, wgT, wa, waT, a, out):
    f32, i32, bf16, f16 = mybir.dt.float32, mybir.dt.int32, mybir.dt.bfloat16, mybir.dt.float16
    ALU, ACT, AX = mybir.AluOpType, mybir.ActivationFunctionType, mybir.AxisListType
    ctx = ExitStack()
    with ctx:
        def sb(name, shape, dt=f32):
            return ctx.enter_context(nc.sbuf_tensor("sb_" + name, shape, dt))

        def sem(name):
            return ctx.enter_context(nc.semaphore(name))

        raw = sb("raw", [P, SLOTS, CT * GW], i32)
        mask = sb("mask", [P, CHUNKS, CT, GW], bf16)
        xs = sb("xs", [P, TILES, F])
        ghi = sb("ghi", [P, TILES, F], f16)
        glo = sb("glo", [P, TILES, F], f16)
        u = raw[:, SLOTS - 2, :].bitcast(f32).rearrange("p (t f) -> p t f", f=F)
        pw = raw[:, SLOTS - 1, :].bitcast(f32).rearrange("p (t f) -> p t f", f=F)
        half = CHUNKS // 2
        tmp = mask[:, 0:half, :, :].rearrange("p a c w -> p (a c w)").bitcast(f32).rearrange(
            "p (t f) -> p t f", f=F)
        uT = mask[:, half:CHUNKS, :, :].rearrange("p a c w -> p (a c w)").bitcast(f32).rearrange(
            "p (t f) -> p t f", f=F)

        hp = sb("hp", [P, GT, F])
        mn = sb("mn", [P, GT, F])
        ident, wge, wgeT, waTs = (hp[:, n, :] for n in range(4))
        spare = mn[:, :, :].rearrange("p t f -> p (t f)")
        ones = sb("ones", [3, P])
        wae = sb("wae", [P, F])
        a2 = sb("a2", [P, 2])
        v2 = sb("v2", [P, 2])
        ws = sb("ws", [P, 1])

        def short(n):
            return spare[:, n * TILES:(n + 1) * TILES]

        def col(name, n=TILES, dt=f32):
            return sb(name, [P, n], dt)

        mean, var, usum, psum2, u0 = (short(n) for n in range(5))
        rr = col("rr", 2 * TILES)
        y = col("y", 2 * TILES)
        yt = col("yt", 2 * TILES)
        tm, z, w, lw, lw2, w2, n2, ep, en, sh, coef = (short(n) for n in range(5, 16))
        nn, rn, t1, t2 = col("nn"), col("rn"), col("t1"), col("t2")
        sd = col("sd", 2 * TILES)
        ss, dd = sd[:, 0:TILES], sd[:, TILES:]
        kap, pp, pw2, qq, gs = col("kap"), col("pp"), col("pw2"), col("qq"), col("gs")
        ext = col("ext", 3)
        extT = sb("extT", [3, 1])
        exd = sb("exd", [3, 3])
        exb = col("exb", 3)
        negD = col("negD", 1)
        hs = col("hs", 1)
        R = sb("R", [1, F])

        numT = sb("numT", [P, GW])
        zr = sb("zr", [1, GW])
        rden = col("rden", GT)
        em = sg = hp
        s1, s2 = col("s1", GT), col("s2", GT)
        erw = col("erw", 2 * GT)
        ey, eyt = col("ey", 2 * GT), col("eyt", 2 * GT)
        etm, ez, ew, elw, ef = (col("etm", GT), col("ez", GT), col("ew", GT), col("elw", GT), col("ef", GT))
        exn, eep, een, esh, ech = col("exn", GT), col("eep", GT), col("een", GT), col("esh", GT), col("ech", GT)
        o = sb("o", [P, GT, F])

        bank = [ctx.enter_context(nc.psum_tensor(f"bank{b}", [P, 512], f32)) for b in range(8)]
        acc = bank[0:2]
        E = bank[2][:, :].rearrange("p (t f) -> p t f", f=F)
        junk = bank[3][:, :].rearrange("p (t f) -> p t f", f=F)
        pT = bank[0:4]
        pP = bank[4:6]
        misc = bank[6]
        pV, pW, pS = misc[:, 0:2], misc[:, 2:4], misc[:, 32:64]
        pE, pB = bank[7][0:3, 0:P], bank[7][:, 256:259]
        pH, pR = bank[4][:, 0:1], bank[5][0:1, 0:F]

        adj_in = [sem(f"adj_in{s}") for s in range(SLOTS)]
        x_in = [sem(f"x_in{k}") for k in range(QUARTERS)]
        w_in = sem("w_in")
        zeroed, id_ready = sem("zeroed"), sem("id_ready")
        centred, squared, var_taken, u_ready = sem("centred"), sem("squared"), sem("var_taken"), sem("u_ready")
        u_squared, u_taken, uT_made, uT_ready = sem("u_squared"), sem("u_taken"), sem("uT_made"), sem("uT_ready")
        v_made, v_copied, w_made, w_copied = sem("v_made"), sem("v_copied"), sem("w_made"), sem("w_copied")
        p_made, p_copied, p_squared = sem("p_made"), sem("p_copied"), sem("p_squared")
        ln_arg, ln_done, n_ready, exps_done = sem("ln_arg"), sem("ln_done"), sem("n_ready"), sem("exps_done")
        kap_ready, ext_ready, extT_made = sem("kap_ready"), sem("ext_ready"), sem("extT_made")
        exd_ready, exb_made, d_ready, p_ready = sem("exd_ready"), sem("exb_made"), sem("d_ready"), sem("p_ready")
        h_summed, hs_ready, r_made, r_ready = sem("h_summed"), sem("hs_ready"), sem("r_made"), sem("r_ready")
        g_ready, hi_ready, lo_ready = sem("g_ready"), sem("hi_ready"), sem("lo_ready")
        prep_done = sem("prep_done")
        masks_ready, masks_used = sem("masks_ready"), sem("masks_used")
        num_ready, e_ready = sem("num_ready"), sem("e_ready")
        mn_ready, ex_ready, em_ready, s1_ready = sem("mn_ready"), sem("ex_ready"), sem("em_ready"), sem("s1_ready")
        ew_ready, elw_ready, ef_ready, s2_ready = sem("ew_ready"), sem("elw_ready"), sem("ef_ready"), sem("s2_ready")
        en_ready, eexp_ready, o_ready = sem("en_ready"), sem("eexp_ready"), sem("o_ready")
        o_stored = sem("o_stored")
        dve_step, act_step = sem("dve_step"), sem("act_step")

        def quarter(k):
            return slice(k * QT, (k + 1) * QT)

        block = ctx.enter_context(nc.Block())

        @block.sync
        def _(sp):
            def load(grp, b, c):
                s = b * CHUNKS + c
                sp.dma_start(raw[:, s, :], adj[grp * CHUNKS + c]).then_inc(adj_in[s], 16)

            def store(grp):
                sp.wait_ge(o_ready, grp + 1)
                sp.dma_start(out[:, grp, :], o[:, :, :].rearrange("p t f -> p (t f)")).then_inc(o_stored, 16)

            for c in range(CHUNKS):
                load(0, 0, c)
            for c in range(CHUNKS):
                if c == CHUNKS - 2:
                    sp.wait_ge(prep_done, 1)
                load(1, 1, c)

            def turn(grp, b):
                for c in range(CHUNKS):
                    sp.wait_ge(masks_ready, grp * CHUNKS + c + 1)
                    load(grp + 2, b, c)
                if not (isinstance(grp, int) and grp == 0):
                    store(grp - 1)

            turn(0, 0)
            with sp.Fori(0, (GROUPS - 4) // 2) as it:
                turn(it * 2 + 1, 1)
                turn(it * 2 + 2, 0)
            turn(GROUPS - 3, 1)
            for g in range(GROUPS - 3, GROUPS):
                store(g)
            sp.wait_ge(o_stored, 16 * (GROUPS + 1))

        @block.gpsimd
        def _(pool):
            pool.memset(ident[:, :], 0.0).then_inc(zeroed, 1)
            pool.wait_ge(zeroed, 1)
            pool.affine_select(out=ident[:, :], in_=ident[:, :], compare_op=ALU.not_equal, fill=1.0, base=0,
                               pattern=[[-1, P]], channel_multiplier=1).then_inc(id_ready, 1)
            pool.memset(ones[:, :], 1.0).then_inc(id_ready, 1)

        @block.scalar
        def _(act):
            step = Chain(act, act_step)

            def keep_products(k):
                act.wait_ge(p_made, k + 1)
                act.wait_ge(u_taken, k + 1)
                for b in range(2):
                    r = slice(k * QT + b * GT, k * QT + (b + 1) * GT)
                    act.activation(pw[:, r, :].rearrange("p t f -> p (t f)"), pP[b][:, :], ACT.Copy)
                    act.activation(tmp[:, r, :].rearrange("p t f -> p (t f)"), pP[b][:, :],
                                   ACT.Square).then_inc(p_squared, 1)

            for k in range(QUARTERS):
                act.dma_start(xs[:, quarter(k), :], x[:, quarter(k), :]).then_inc(x_in[k], 16)
                if k == 0:
                    act.dma_start(waTs[:, :], waT).then_inc(w_in, 16)
                    act.dma_start(a2[:, :], a).then_inc(w_in, 16)
                    act.wait_ge(v_copied, 1)
                    act.dma_start(wge[1:P, 1:F], wg).then_inc(w_in, 16)
                    act.dma_start(wgeT[1:P, 1:F], wgT).then_inc(w_in, 16)
                    act.dma_start(wae[1:P, 1:F], wa[1:P, 1:F]).then_inc(w_in, 16)
            for k in range(QUARTERS):
                q = quarter(k)
                act.wait_ge(centred, k + 1)
                act.activation(tmp[:, q, :], u[:, q, :], ACT.Square).then_inc(squared, 1)
                act.wait_ge(squared, k + 1)
                act.activation(u[:, q, :], u[:, q, :], ACT.Relu).then_inc(u_ready, 1)
            for k in range(QUARTERS):
                q = quarter(k)
                act.wait_ge(var_taken, k + 1)
                act.wait_ge(u_ready, k + 1)
                act.activation(tmp[:, q, :], u[:, q, :], ACT.Square).then_inc(u_squared, 1)
                act.wait_ge(uT_made, k + 1)
                for b in range(2):
                    act.activation(uT[:, k * QT + b * GT:k * QT + (b + 1) * GT, :].rearrange("p t f -> p (t f)"),
                                   pT[k % 2 * 2 + b][:, :], ACT.Copy).then_inc(uT_ready, 1)
                if k >= 1:
                    keep_products(k - 1)
            keep_products(QUARTERS - 1)

            act.wait_ge(ln_arg, 1)
            act.activation(lw[:, :], w[:, :], ACT.Ln).then_inc(ln_done, 1)
            act.wait_ge(n_ready, 1)
            act.activation(ep[:, :], nn[:, :], ACT.Exp)
            act.activation(en[:, :], nn[:, :], ACT.Exp, scale=-1.0).then_inc(exps_done, 1)
            act.wait_ge(ln_arg, 2)
            act.activation(lw[:, :], w[:, :], ACT.Ln)
            act.activation(lw2[:, :], w2[:, :], ACT.Ln).then_inc(ln_done, 1)
            act.wait_ge(d_ready, 1)
            act.activation(pp[:, :], dd[:, :], ACT.Exp, bias=negD[:, :]).then_inc(p_ready, 1)
            for k in range(QUARTERS):
                q = quarter(k)
                act.wait_ge(g_ready, k + 1)
                act.activation(ghi[:, q, :], tmp[:, q, :], ACT.Copy).then_inc(hi_ready, 1)

            def finish(grp):
                act.wait_ge(masks_used, (grp + 2) * CHUNKS)
                act.activation(numT[:, :], acc_of(grp), ACT.Copy)
                act.activation(zr[:, :], acc_of(grp)[0:1, :], ACT.Relu, bias=1.0,
                               scale=-1e34).then_inc(num_ready, 1)
                act.wait_ge(mn_ready, grp + 1)
                act.activation(mn[:, :, :], mn[:, :, :], ACT.Exp).then_inc(ex_ready, 1)
                act.wait_ge(em_ready, grp + 1)
                for t in range(GT):
                    last = act.activation(junk[:, t, 1:F], em[:, t, 1:F], ACT.Square, accum_out=s1[:, t:t + 1])
                last.then_inc(s1_ready, 1)
                act.wait_ge(ew_ready, grp + 1)
                act.activation(elw[:, :], ew[:, :], ACT.Ln).then_inc(elw_ready, 1)
                act.wait_ge(ef_ready, grp + 1)
                for t in range(GT):
                    last = act.activation(sg[:, t, 1:F], em[:, t, 1:F], ACT.Sigmoid, scale=ef[:, t:t + 1])
                step(last)
                for t in range(GT):
                    last = act.activation(junk[:, t, 1:F], sg[:, t, 1:F], ACT.Square, accum_out=s2[:, t:t + 1])
                last.then_inc(s2_ready, 1)
                act.wait_ge(en_ready, grp + 1)
                act.activation(eep[:, :], exn[:, :], ACT.Exp)
                act.activation(een[:, :], exn[:, :], ACT.Exp, scale=-1.0).then_inc(eexp_ready, 1)

            parity = [0]

            def acc_of(grp):
                return acc[parity[0]][:, :]

            with act.Fori(0, GROUPS // 2) as it:
                step.enter(it, 2)
                for b in range(2):
                    parity[0] = b
                    finish(it * 2 + b)
                step.leave(GROUPS // 2)

        @block.vector
        def _(dve):
            step = Chain(dve, dve_step)

            def rsqrt(res, arg, tmp_, n):
                r, v, t = res[:, 0:n], arg[:, 0:n], tmp_[:, 0:n]
                step(dve.tensor_scalar(r.bitcast(i32), v.bitcast(i32), 1, None, ALU.logical_shift_right))
                step(dve.tensor_scalar(r.bitcast(i32), r.bitcast(i32), -1.0, float(RSQRT_SEED), ALU.mult, ALU.add))
                for _ in range(3):
                    step(dve.scalar_tensor_tensor(t, r, -0.5, v, ALU.mult, ALU.mult))
                    step(dve.tensor_tensor(t, t, r, ALU.mult))
                    step(dve.scalar_tensor_tensor(r, t, 1.5, r, ALU.add, ALU.mult))

            dve.memset(wge[:, :], 0.0)
            dve.memset(wgeT[:, :], 0.0)
            step(dve.memset(wae[:, :], 0.0))
            dve.memset(wae[0:1, 0:1], 1.0).then_inc(v_copied, 1)
            dve.memset(zr[:, :], 0.0).then_inc(masks_used, CHUNKS)
            dve.memset(rden[:, :], 0.0).then_inc(o_stored, 16)

            for k in range(QUARTERS):
                q = quarter(k)
                dve.wait_ge(x_in[k], 16)
                step(dve.tensor_reduce(mean[:, q], xs[:, q, :], AX.X, ALU.add))
                step(dve.tensor_scalar(mean[:, q], mean[:, q], 1.0 / F, None, ALU.mult))
                dve.tensor_tensor(u[:, q, :], xs[:, q, :], mean[:, q].unsqueeze(2).to_broadcast([P, QT, F]),
                                  ALU.subtract).then_inc(centred, 1)
                if k == 0:
                    dve.wait_ge(v_made, 1)
                    dve.tensor_copy(v2[:, :], pV).then_inc(v_copied, 1)
                    dve.wait_ge(w_made, 1)
                    dve.tensor_copy(wge[:, 0:1], pW[:, 1:2]).then_inc(w_copied, 1)
                    dve.tensor_copy(ws[:, :], pW[:, 0:1]).then_inc(w_copied, 1)
            for k in range(QUARTERS):
                q = quarter(k)
                dve.wait_ge(squared, k + 1)
                dve.tensor_reduce(var[:, q], tmp[:, q, :], AX.X, ALU.add).then_inc(var_taken, 1)
            for k in range(QUARTERS):
                q = quarter(k)
                dve.wait_ge(u_squared, k + 1)
                dve.tensor_reduce(usum[:, q], tmp[:, q, 1:F], AX.X, ALU.add).then_inc(u_taken, 1)
                dve.wait_ge(u_ready, k + 1)
                step(dve.tensor_copy(u0[:, q], u[:, q, 0]))

            step(dve.tensor_scalar(rr[:, 0:TILES], var[:, :], 1.0 / F, 1e-5, ALU.mult, ALU.add))
            step(dve.reciprocal(var[:, :], rr[:, 0:TILES]))
            step(dve.tensor_tensor(rr[:, TILES:], usum[:, :], var[:, :], ALU.mult))
            step(dve.tensor_scalar(rr[:, TILES:], rr[:, TILES:], 1e-30, None, ALU.max))
            rsqrt(y, rr, yt, 2 * TILES)
            step(dve.tensor_tensor(tm[:, :], u0[:, :], y[:, 0:TILES], ALU.mult))
            dve.tensor_tensor(coef[:, :], y[:, 0:TILES], y[:, TILES:], ALU.mult)
            step(dve.tensor_scalar(tm[:, :], tm[:, :], -1.0, EPS, ALU.add, ALU.max))
            step(dve.scalar_tensor_tensor(rr[:, 0:TILES], tm[:, :], 2.0, tm[:, :], ALU.add, ALU.mult))
            rsqrt(y, rr, yt, TILES)
            step(dve.tensor_tensor(z[:, :], rr[:, 0:TILES], y[:, 0:TILES], ALU.mult))
            step(dve.tensor_tensor(z[:, :], tm[:, :], z[:, :], ALU.add))
            step(dve.tensor_scalar(w[:, :], z[:, :], 1.0, None, ALU.add))

            def log1p_rest(res, z_, w_, lw_):
                step(dve.tensor_scalar(w_, w_, -1.0, None, ALU.add))
                step(dve.reciprocal(w_, w_))
                step(dve.tensor_tensor(z_, z_, w_, ALU.mult))
                step(dve.tensor_tensor(res, lw_, z_, ALU.mult))

            dve.sem_inc(ln_arg, 1)
            for k in range(QUARTERS):
                q = quarter(k)
                dve.wait_ge(p_squared, 2 * k + 2)
                step(dve.tensor_reduce(psum2[:, q], tmp[:, q, 1:F], AX.X, ALU.add))
            dve.wait_ge(ln_done, 1)
            log1p_rest(t1[:, :], z[:, :], w[:, :], lw[:, :])
            step(dve.tensor_tensor(coef[:, :], coef[:, :], t1[:, :], ALU.mult))
            step(dve.tensor_tensor(n2[:, :], coef[:, :], coef[:, :], ALU.mult))
            step(dve.tensor_tensor(n2[:, :], n2[:, :], psum2[:, :], ALU.mult))
            step(dve.tensor_scalar(n2[:, :], n2[:, :], 1e-30, None, ALU.max))
            rsqrt(rn, n2, yt, TILES)
            step(dve.tensor_tensor(nn[:, :], n2[:, :], rn[:, :], ALU.mult))
            dve.sem_inc(n_ready, 1)
            step(dve.tensor_scalar(t1[:, :], n2[:, :], 1.0 / 42.0, 1.0, ALU.mult, ALU.add))
            step(dve.scalar_tensor_tensor(t1[:, :], t1[:, :], 1.0 / 20.0, n2[:, :], ALU.mult, ALU.mult))
            step(dve.scalar_tensor_tensor(t1[:, :], t1[:, :], 1.0, n2[:, :], ALU.add, ALU.mult))
            step(dve.tensor_scalar(t1[:, :], t1[:, :], 1.0 / 6.0, 1.0, ALU.mult, ALU.add))
            step(dve.tensor_tensor(t1[:, :], t1[:, :], nn[:, :], ALU.mult))
            step(dve.scalar_tensor_tensor(t1[:, :], n2[:, :], 0.25, t1[:, :], ALU.is_lt, ALU.mult))
            dve.wait_ge(exps_done, 1)
            step(dve.tensor_tensor(t2[:, :], ep[:, :], en[:, :], ALU.subtract))
            step(dve.tensor_scalar(t2[:, :], t2[:, :], 0.5, None, ALU.mult))
            step(dve.scalar_tensor_tensor(t2[:, :], n2[:, :], 0.25, t2[:, :], ALU.is_ge, ALU.mult))
            step(dve.tensor_tensor(sh[:, :], t1[:, :], t2[:, :], ALU.add))
            step(dve.tensor_tensor(t1[:, :], sh[:, :], sh[:, :], ALU.mult))
            step(dve.tensor_scalar(rr[:, 0:TILES], t1[:, :], 1.0, None, ALU.add))
            rsqrt(y, rr, yt, TILES)
            step(dve.tensor_tensor(t2[:, :], rr[:, 0:TILES], y[:, 0:TILES], ALU.mult))
            step(dve.tensor_scalar(t2[:, :], t2[:, :], 1.0, None, ALU.add))
            step(dve.reciprocal(t2[:, :], t2[:, :]))
            step(dve.tensor_tensor(tm[:, :], t1[:, :], t2[:, :], ALU.mult))
            step(dve.tensor_scalar(tm[:, :], tm[:, :], EPS, None, ALU.max))
            step(dve.scalar_tensor_tensor(z[:, :], sh[:, :], ROOT_EPS, tm[:, :], ALU.max, ALU.add))
            step(dve.tensor_scalar(t1[:, :], z[:, :], 1.0, None, ALU.add))
            step(dve.tensor_scalar(w[:, :], t1[:, :], 2.0 ** 60, None, ALU.min))
            step(dve.tensor_scalar(w2[:, :], t1[:, :], 2.0 ** -60, 1.0, ALU.mult, ALU.max))
            dve.sem_inc(ln_arg, 1)
            dve.wait_ge(ln_done, 2)
            step(dve.tensor_tensor(lw[:, :], lw[:, :], lw2[:, :], ALU.add))
            log1p_rest(kap[:, :], z[:, :], t1[:, :], lw[:, :])
            step(dve.tensor_tensor(kap[:, :], kap[:, :], coef[:, :], ALU.mult))
            step(dve.tensor_tensor(kap[:, :], kap[:, :], rn[:, :], ALU.mult))
            dve.sem_inc(kap_ready, 1)
            dve.tensor_tensor(dd[:, :], kap[:, :], pw[:, :, 0], ALU.mult)
            step(dve.tensor_tensor(ss[:, :], kap[:, :], pS, ALU.mult))
            dve.tensor_reduce(ext[:, 0:1], dd[:, :], AX.X, ALU.max)
            step(dve.tensor_scalar(t1[:, :], dd[:, :], -1.0, None, ALU.mult))
            dve.tensor_reduce(ext[:, 1:2], t1[:, :], AX.X, ALU.max)
            dve.tensor_reduce(ext[:, 2:3], sd[:, :], AX.X, ALU.max, apply_absolute_value=True).then_inc(ext_ready, 1)
            dve.wait_ge(extT_made, 1)
            step(dve.tensor_reduce(extT[:, :], pE, AX.X, ALU.max))
            dve.tensor_scalar(exd[:, :], ident[0:3, 0:3], extT[:, 0:1], None, ALU.mult).then_inc(exd_ready, 1)
            dve.wait_ge(exb_made, 1)
            dve.tensor_scalar(negD[:, :], pB[:, 0:1], -1.0, None, ALU.mult).then_inc(d_ready, 1)
            dve.tensor_copy(exb[:, :], pB)
            dve.wait_ge(p_ready, 1)
            step(dve.tensor_scalar(pw2[:, :].bitcast(i32), pp[:, :].bitcast(i32), 0x7F800000, None,
                                   ALU.bitwise_and))
            step(dve.tensor_scalar(qq[:, :].bitcast(i32), pp[:, :].bitcast(i32), 0x007FFFFF, 0x3F800000,
                                   ALU.bitwise_and, ALU.bitwise_or))
            step(dve.tensor_scalar(qq[:, :], qq[:, :], G_SCALE, None, ALU.mult))
            step(dve.tensor_tensor(gs[:, :], qq[:, :], kap[:, :], ALU.mult))
            for k in range(QUARTERS):
                q = quarter(k)
                step(dve.tensor_tensor(tmp[:, q, :], pw[:, q, :], gs[:, q].unsqueeze(2).to_broadcast([P, QT, F]),
                                       ALU.mult))
                dve.tensor_copy(tmp[:, q, 0], qq[:, q]).then_inc(g_ready, 1)
            for k in range(QUARTERS):
                q = quarter(k)
                dve.wait_ge(hi_ready, k + 1)
                dve.tensor_tensor(glo[:, q, :], tmp[:, q, :], ghi[:, q, :], ALU.subtract).then_inc(lo_ready, 1)
            dve.wait_ge(h_summed, 1)
            step(dve.tensor_copy(hs[:, :], pH))
            dve.memset(hs[0:1, :], float(N)).then_inc(hs_ready, 1)
            dve.wait_ge(r_made, 1)
            dve.wait_ge(lo_ready, QUARTERS)
            dve.tensor_copy(R[:, :], pR).then_inc(r_ready, 1)
            dve.wait_ge(r_ready, 1)
            dve.sem_inc(prep_done, 1)

            def masks(grp, b, c, lo, hi):
                s = b * CHUNKS + c
                if lo == 0:
                    dve.wait_ge(adj_in[s], (grp - b) * 8 + 16)
                    dve.wait_ge(masks_used, grp * CHUNKS + c + 1)
                for n in range(lo, hi):
                    j = c * CT + n
                    last = dve.tensor_scalar(mask[:, c, n, :], raw[:, s, n * GW:(n + 1) * GW], 0.0,
                                             pw2[:, j:j + 1], ALU.is_gt, ALU.mult)
                if hi == CT:
                    last.then_inc(masks_ready, 1)

            def divide(grp):
                dve.wait_ge(e_ready, grp + 1)
                step(dve.reciprocal(rden[:, :], E[:, :, 0]))
                step(dve.tensor_tensor(hp[:, :, :], E, rden[:, :].unsqueeze(2).to_broadcast([P, GT, F]), ALU.mult))
                dve.tensor_scalar(mn[:, :, :], hp[:, :, :], 0.0, None, ALU.min).then_inc(mn_ready, 1)

            def elu(grp):
                dve.wait_ge(ex_ready, grp + 1)
                dve.scalar_tensor_tensor(em[:, :, :], mn[:, :, :], -1.0, hp[:, :, :], ALU.add,
                                         ALU.max).then_inc(em_ready, 1)

            def log_arg(grp):
                dve.wait_ge(s1_ready, grp + 1)
                dve.tensor_scalar(erw[:, 0:GT], s1[:, :], 1.0, None, ALU.add)
                step(dve.tensor_scalar(erw[:, GT:], s1[:, :], 1e-30, None, ALU.max))
                rsqrt(ey, erw, eyt, 2 * GT)
                step(dve.tensor_tensor(erw[:, :], erw[:, :], ey[:, :], ALU.mult))
                step(dve.tensor_scalar(etm[:, :], erw[:, 0:GT], 1.0, None, ALU.add))
                step(dve.reciprocal(etm[:, :], etm[:, :]))
                step(dve.tensor_tensor(etm[:, :], s1[:, :], etm[:, :], ALU.mult))
                step(dve.tensor_scalar(etm[:, :], etm[:, :], EPS, None, ALU.max))
                step(dve.scalar_tensor_tensor(ez[:, :], erw[:, GT:], ROOT_EPS, etm[:, :], ALU.max, ALU.add))
                dve.tensor_scalar(ew[:, :], ez[:, :], 1.0, None, ALU.add).then_inc(ew_ready, 1)

            def log_scale(grp):
                dve.wait_ge(elw_ready, grp + 1)
                log1p_rest(ef[:, :], ez[:, :], ew[:, :], elw[:, :])
                dve.tensor_tensor(ef[:, :], ef[:, :], ey[:, GT:], ALU.mult).then_inc(ef_ready, 1)

            def out_norm(grp):
                dve.wait_ge(s2_ready, grp + 1)
                step(dve.tensor_scalar(erw[:, 0:GT], s2[:, :], 1e-30, None, ALU.max))
                rsqrt(ey, erw, eyt, GT)
                dve.tensor_tensor(exn[:, :], erw[:, 0:GT], ey[:, 0:GT], ALU.mult).then_inc(en_ready, 1)

            def output(grp):
                dve.wait_ge(eexp_ready, grp + 1)
                dve.tensor_tensor(ech[:, :], eep[:, :], een[:, :], ALU.add)
                step(dve.tensor_tensor(esh[:, :], eep[:, :], een[:, :], ALU.subtract))
                step(dve.tensor_scalar(esh[:, :], esh[:, :], 0.5, None, ALU.mult))
                dve.wait_ge(o_stored, grp * 16 + 16)
                step(dve.tensor_tensor(esh[:, :], esh[:, :], ey[:, 0:GT], ALU.mult))
                for t in range(GT):
                    dve.scalar_tensor_tensor(o[:, t, 1:F], sg[:, t, 1:F], esh[:, t:t + 1],
                                             xs[:, grp * GT + t, 1:F], ALU.mult, ALU.add)
                dve.scalar_tensor_tensor(o[:, :, 0], ech[:, :], 0.5,
                                         xs[:, bass.ds(grp * GT, GT), 0], ALU.mult, ALU.add).then_inc(o_ready, 1)

            def rows(grp, b, before):
                masks(grp, b, 0, 0, CT)
                masks(grp, b, 1, 0, 4)
                if before:
                    divide(grp - 1)
                masks(grp, b, 1, 4, CT)
                if before:
                    elu(grp - 1)
                masks(grp, b, 2, 0, 4)
                if before:
                    log_arg(grp - 1)
                masks(grp, b, 2, 4, 6)
                if before:
                    log_scale(grp - 1)
                masks(grp, b, 2, 6, CT)
                masks(grp, b, 3, 0, 4)
                if before:
                    out_norm(grp - 1)
                masks(grp, b, 3, 4, 6)
                if before:
                    output(grp - 1)
                masks(grp, b, 3, 6, CT)

            rows(0, 0, False)
            with dve.Fori(0, (GROUPS - 2) // 2) as it:
                step.enter(it, 2 * STEPS)
                rows(it * 2 + 1, 1, True)
                rows(it * 2 + 2, 0, True)
                step.leave((GROUPS - 2) // 2)
            g = GROUPS - 1
            rows(g, g % 2, True)
            divide(g)
            elu(g)
            log_arg(g)
            log_scale(g)
            out_norm(g)
            output(g)

        @block.tensor
        def _(pe):
            pe.wait_ge(id_ready, 2)
            pe.wait_ge(w_in, 5 * 16)
            pe.matmul(pV, waTs[:, :], a2[:, :], start=True, stop=True).then_inc(v_made, 1)
            pe.wait_ge(v_copied, 2)
            pe.matmul(pW, wgeT[:, :], v2[:, :], start=True, stop=True).then_inc(w_made, 1)

            def transposes(k):
                pe.wait_ge(u_ready, k + 1)
                if k >= 2:
                    pe.wait_ge(uT_ready, 2 * (k - 1))
                for n in range(QT):
                    last = pe.transpose(pT[k % 2 * 2 + n // GT][:, n % GT * P:(n % GT + 1) * P],
                                        u[:, k * QT + n, :], ident[:, :])
                last.then_inc(uT_made, 1)

            def products(k):
                pe.wait_ge(uT_ready, 2 * k + 2)
                if k == 0:
                    pe.wait_ge(w_copied, 2)
                else:
                    pe.wait_ge(p_squared, 2 * k)
                for n in range(QT):
                    t = k * QT + n
                    pe.matmul(pS[:, t:t + 1], uT[:, t, :], ws[:, :], start=True, stop=True)
                    last = pe.matmul(pP[n // GT][:, n % GT * F:(n % GT + 1) * F], uT[:, t, :], wge[:, :],
                                     start=True, stop=True)
                last.then_inc(p_made, 1)

            transposes(0)
            for k in range(1, QUARTERS):
                transposes(k)
                products(k - 1)
            products(QUARTERS - 1)

            pe.wait_ge(kap_ready, 1)
            pe.wait_ge(p_squared, 2 * QUARTERS)
            for t in range(TILES):
                last = pe.matmul(pH, pw[:, t, :], kap[:, t:t + 1], start=(t == 0), stop=(t == TILES - 1))
                if t == 0:
                    pass
            last.then_inc(h_summed, 1)
            pe.wait_ge(ext_ready, 1)
            pe.transpose(pE, ext[:, :], ident[:, :]).then_inc(extT_made, 1)
            pe.wait_ge(exd_ready, 1)
            pe.matmul(pB, ones[:, :], exd[:, :], start=True, stop=True).then_inc(exb_made, 1)
            pe.wait_ge(hs_ready, 1)
            pe.matmul(pR, hs[:, :], wae[:, :], start=True, stop=True).then_inc(r_made, 1)
            pe.wait_ge(prep_done, 1)

            def gather(grp, b, c):
                pe.wait_ge(masks_ready, grp * CHUNKS + c + 1)
                for n in range(CT):
                    j = c * CT + n
                    pe.matmul(acc[b][:, :], ghi[:, j, :], mask[:, c, n, :], start=(j == 0), stop=False)
                    last = pe.matmul(acc[b][:, :], glo[:, j, :], mask[:, c, n, :], start=False,
                                     stop=(j == TILES - 1))
                last.then_inc(masks_used, 1)

            def attend(grp):
                pe.wait_ge(num_ready, grp + 1)
                for t in range(GT):
                    pe.matmul(E[:, t, :], numT[:, t * P:(t + 1) * P], wae[:, :], start=True, stop=False)
                    last = pe.matmul(E[:, t, :], zr[0:1, t * P:(t + 1) * P], R[0:1, :], start=False, stop=True)
                last.then_inc(e_ready, 1)

            def group(grp, b, before):
                gather(grp, b, 0)
                if before:
                    attend(grp - 1)
                for c in range(1, CHUNKS):
                    gather(grp, b, c)

            group(0, 0, False)
            with pe.Fori(0, (GROUPS - 2) // 2) as it:
                group(it * 2 + 1, 1, True)
                group(it * 2 + 2, 0, True)
            g = GROUPS - 1
            group(g, g % 2, True)
            attend(g)


STEPS = 39


def kernel(**inputs):
    import numpy as np
    import concourse.bacc as bacc
    from concourse.bass_utils import run_bass_kernel_spmd

    f = np.ascontiguousarray
    adj = np.asarray(inputs["adj"]).reshape(P, GROUPS, GT, P, CHUNKS, CT)
    adj = f(adj.transpose(1, 4, 3, 5, 2, 0)).reshape(GROUPS * CHUNKS, P, CT * GW)
    wg, wa = np.asarray(inputs["L0_gnn_W_gcn"]), np.asarray(inputs["L0_gnn_W_att"])
    arrays = {
        "x": f(inputs["x"]).reshape(P, TILES, F),
        "adj": adj,
        "wg": f(wg), "wgT": f(wg.T), "wa": f(wa), "waT": f(wa.T),
        "a": f(np.asarray(inputs["L0_gnn_a_att"]).reshape(2, F).T),
    }
    nc = bacc.Bacc("TRN2", target_bir_lowering=False, num_devices=1)
    args = [nc.dram_tensor(n, v.shape, mybir.dt.from_np(v.dtype), kind="ExternalInput").ap()
            for n, v in arrays.items()]
    out = nc.dram_tensor("out", (P, GROUPS, GT * F), mybir.dt.float32, kind="ExternalOutput").ap()
    layer(nc, *args, out)
    r = run_bass_kernel_spmd(nc, [arrays], core_ids=[0])
    return r.results[0]["out"].reshape(N, F)
```

```python
import concourse.bass as bass
from concourse import mybir
from contextlib import ExitStack

P = 128
N = 4096
F = 128
TILES = N // P
SLOT = 4096
SLOTS = 8
RING = 4
WIDE, NARROW = 8, 4
WIDES, NARROWS = 3, 2
GROUPS = WIDES + NARROWS
CHUNKS = TILES * N // SLOT
BANK = 512
BT = BANK // F
QUARTERS = 4
QT = TILES // QUARTERS
EPS = 2.0 ** -23
ROOT_EPS = (EPS * (EPS + 2.0)) ** 0.5
G_SCALE = 512.0


class Chain:

    def __init__(self, eng, sem):
        self.eng, self.sem, self.base, self.n = eng, sem, 0, 0

    def __call__(self, ins):
        self.n += 1
        ins.then_inc(self.sem, 1)
        self.eng.wait_ge(self.sem, self.base + self.n)

    def enter(self, it, per):
        self.before, self.per = self.n, per
        self.base, self.n = it * per + self.before, 0

    def leave(self, trips):
        assert self.n == self.per, self.n
        self.base, self.n = 0, self.before + trips * self.per


def layer(nc, x, adj, wg, wgT, wa, waT, a, out):
    f32, i32, bf16, f16 = mybir.dt.float32, mybir.dt.int32, mybir.dt.bfloat16, mybir.dt.float16
    ALU, ACT, AX = mybir.AluOpType, mybir.ActivationFunctionType, mybir.AxisListType
    ctx = ExitStack()
    with ctx:
        def sb(name, shape, dt=f32):
            return ctx.enter_context(nc.sbuf_tensor("sb_" + name, shape, dt))

        def sem(name):
            return ctx.enter_context(nc.semaphore(name))

        raw = sb("raw", [P, SLOTS, SLOT], i32)
        mask = sb("mask", [P, RING, SLOT], bf16)
        xs = sb("xs", [P, TILES, F])
        ghi = sb("ghi", [P, TILES, F], f16)
        glo = sb("glo", [P, TILES, F], f16)
        half = RING // 2
        u, pw = (mask[:, h * half:(h + 1) * half, :].rearrange("p a w -> p (a w)").bitcast(f32).rearrange(
            "p (t f) -> p t f", f=F) for h in range(2))
        tmp = raw[:, SLOTS - 1, :].bitcast(f32).rearrange("p (t f) -> p t f", f=F)
        nat = ghi[:, :, :].rearrange("p (b s t) f -> p b s t f", b=2, s=2)
        uT = glo[:, :, :].rearrange("p (b s t) f -> p b s t f", b=2, s=2)

        hp = sb("hp", [P, WIDE, F])
        mn = sb("mn", [P, WIDE, F])
        numT = mn[:, :, :].rearrange("p t f -> p (t f)")
        wge, wgeT, waTs, idf = (hp[:, n, :] for n in range(4))
        ident = hp[:, 4, 0:F // 2].bitcast(f16)
        wrest = hp[:, 5, :]
        stats = hp[:, 6:8, :].rearrange("p t f -> p (t f)")[:, 0:6 * TILES].rearrange("p (t s) -> p t s", s=6)
        wparts = sb("wparts", [P, 3, F], bf16)
        spare = numT
        ones = sb("ones", [3, P])
        wae = sb("wae", [P, F])
        a2 = sb("a2", [P, 2])
        v2 = sb("v2", [P, 2])

        def short(n):
            return spare[:, n * TILES:(n + 1) * TILES]

        def col(name, n=TILES, dt=f32):
            return sb(name, [P, n], dt)

        mean, var, usum, psum2, rstd = (short(n) for n in range(5))
        rr = spare[:, 26 * TILES:28 * TILES]
        y = spare[:, 28 * TILES:30 * TILES]
        tm, z, w, lw, lw2, w2, n2, ep, en, sh, coef = (short(n) for n in range(5, 16))
        nn, rn, t1, t2, kap, dd, pp, qq, iq, gs = (short(n) for n in range(16, 26))
        pw2 = col("pw2")
        ext = col("ext", 3)
        extT = sb("extT", [3, 1])
        exd = sb("exd", [3, 3])
        exb = col("exb", 3)
        negD = col("negD", 1)
        hr = sb("hr", [1, F])
        hs = col("hs", 1)
        R = sb("R", [1, 3, F], bf16)
        rf = sb("rf", [1, F])

        zr = sb("zr", [1, WIDE * P], bf16)
        rden = col("rden", WIDE)
        s1, s2, erw, ey = col("s1", WIDE), col("s2", WIDE), col("erw", 2 * WIDE), col("ey", 2 * WIDE)
        eth, etm, ez, ew, elw, ef = (col(n, WIDE) for n in ("eth", "etm", "ez", "ew", "elw", "ef"))
        exn, eep, een, esh, ech = (col(n, WIDE) for n in ("exn", "eep", "een", "esh", "ech"))

        bank = [ctx.enter_context(nc.psum_tensor(f"bank{b}", [P, 512], f32)) for b in range(8)]
        acc = bank[0:2]
        E = [bank[b][:, :].rearrange("p (t f) -> p t f", f=F) for b in (2, 3)]
        junk = [bank[b][:, :].rearrange("p (t f) -> p t f", f=F) for b in (4, 5)]
        pT = bank[0:4]
        pP = bank[4:6]
        misc = bank[6]
        pV, pW = misc[:, 0:2], misc[:, 2:4]
        pE, pB = bank[7][0:3, 0:P], bank[7][:, 256:259]
        pH, pC, pR = bank[6][0:1, 128:128 + F], bank[7][:, 384:385], bank[6][0:1, 384:384 + F]

        adj_in = [sem(f"adj_in{s}") for s in range(SLOTS)]
        x_in = [sem(f"x_in{k}") for k in range(QUARTERS)]
        w_in = sem("w_in")
        zeroed, id_ready = sem("zeroed"), sem("id_ready")
        rstd_arg, rstd_ready, normed, u_ready = sem("rstd_arg"), sem("rstd_ready"), sem("normed"), sem("u_ready")
        hi_made, nat_ready = sem("hi_made"), sem("nat_ready")
        u_squared, u_taken, uT_made, uT_ready = sem("u_squared"), sem("u_taken"), sem("uT_made"), sem("uT_ready")
        v_made, v_copied, w_made, w_copied = sem("v_made"), sem("v_copied"), sem("w_made"), sem("w_copied")
        split = sem("split")
        p_made, p_squared = sem("p_made"), sem("p_squared")
        root_arg, root_done = sem("root_arg"), sem("root_done")
        ln_arg, ln_done, exps_done = sem("ln_arg"), sem("ln_done"), sem("exps_done")
        ext_ready, extT_made = sem("ext_ready"), sem("extT_made")
        exd_ready, exb_made, d_ready, p_ready = sem("exd_ready"), sem("exb_made"), sem("d_ready"), sem("p_ready")
        h_summed, hr_ready, hs_made = sem("h_summed"), sem("hr_ready"), sem("hs_made")
        hs_ready, r_made, r_ready = sem("hs_ready"), sem("r_made"), sem("r_ready")
        g_ready, hi_ready, lo_ready = sem("g_ready"), sem("hi_ready"), sem("lo_ready")
        tmp_free = sem("tmp_free")
        masks_ready, masks_used = sem("masks_ready"), sem("masks_used")
        num_ready, e_ready = sem("num_ready"), sem("e_ready")
        mn_ready, ex_ready, em_ready, s1_ready = sem("mn_ready"), sem("ex_ready"), sem("em_ready"), sem("s1_ready")
        erw_ready, ey_ready, ez_ready = sem("erw_ready"), sem("ey_ready"), sem("ez_ready")
        elw_ready, ef_ready, eexp_ready, o_ready = sem("elw_ready"), sem("ef_ready"), sem("eexp_ready"), sem("o_ready")
        o_stored = sem("o_stored")
        dve_step, act_step = sem("dve_step"), sem("act_step")

        def quarter(k):
            return slice(k * QT, (k + 1) * QT)

        block = ctx.enter_context(nc.Block())

        @block.sync
        def _(sp):
            for k in range(QUARTERS):
                sp.dma_start(xs[:, quarter(k), :], x[:, quarter(k), :]).then_inc(x_in[k], 16)
                if k == 0:
                    sp.wait_ge(v_copied, 1)
                    sp.dma_start(wge[1:P, 1:F], wg).then_inc(w_in, 16)

            def load(n, s):
                sp.dma_start(raw[:, s, :], adj[n]).then_inc(adj_in[s], 16)

            def store(grp, t0, nt):
                sp.wait_ge(o_ready, grp + 1)
                sp.dma_start(out[:, bass.ds(t0 * F, nt * F)],
                             hp[:, 0:nt, :].rearrange("p t f -> p (t f)")).then_inc(o_stored, 16)

            for s in range(SLOTS):
                if s == SLOTS - 1:
                    sp.wait_ge(tmp_free, 1)
                load(s, s)
            for s in range(SLOTS):
                sp.wait_ge(masks_ready, s + 1)
                load(SLOTS + s, s)
            with sp.Fori(1, WIDES) as g:
                for s in range(SLOTS):
                    sp.wait_ge(masks_ready, g * SLOTS + s + 1)
                    load(g * SLOTS + SLOTS + s, s)
                store(g - 1, (g - 1) * WIDE, WIDE)
            store(WIDES - 1, (WIDES - 1) * WIDE, WIDE)
            for n in range(NARROWS):
                store(WIDES + n, WIDES * WIDE + n * NARROW, NARROW)
            sp.wait_ge(o_stored, 16 * (GROUPS + 1))

        @block.gpsimd
        def _(pool):
            pool.memset(idf, 0.0).then_inc(zeroed, 1)
            pool.wait_ge(zeroed, 1)
            pool.affine_select(out=idf, in_=idf, compare_op=ALU.not_equal, fill=1.0, base=0,
                               pattern=[[-1, P]], channel_multiplier=1).then_inc(zeroed, 1)
            pool.memset(ones[:, :], 1.0).then_inc(id_ready, 1)
            pool.wait_ge(zeroed, 2)
            pool.tensor_copy(ident, idf).then_inc(id_ready, 1)
            pool.wait_ge(w_copied, 1)
            pool.wait_ge(w_in, 5 * 16)
            pool.tensor_copy(wparts[:, 0, :], wge).then_inc(split, 1)
            pool.wait_ge(split, 1)
            pool.tensor_tensor(wrest, wge, wparts[:, 0, :], ALU.subtract).then_inc(split, 1)
            pool.wait_ge(split, 2)
            pool.tensor_copy(wparts[:, 1, :], wrest).then_inc(split, 1)
            pool.wait_ge(split, 3)
            pool.tensor_tensor(wrest, wrest, wparts[:, 1, :], ALU.subtract).then_inc(split, 1)
            pool.wait_ge(split, 4)
            pool.tensor_copy(wparts[:, 2, :], wrest).then_inc(split, 1)

        @block.scalar
        def _(act):
            step = Chain(act, act_step)

            def relu(k):
                act.wait_ge(normed, k + 1)
                act.activation(u[:, quarter(k), :], u[:, quarter(k), :], ACT.Relu).then_inc(u_ready, 1)

            def square(k):
                act.wait_ge(u_ready, k + 1)
                act.activation(tmp[:, quarter(k), :], u[:, quarter(k), :], ACT.Square).then_inc(u_squared, 1)

            def keep_transposes(k):
                act.wait_ge(uT_made, k + 1)
                if k >= 2:
                    act.wait_ge(p_made, k - 1)
                for part in range(2):
                    act.activation(uT[:, k % 2, part, :, :].rearrange("p t f -> p (t f)"),
                                   pT[k % 2 * 2 + part][:, :].bitcast(f16), ACT.Copy).then_inc(uT_ready, 1)

            def keep_products(k):
                act.wait_ge(p_made, k + 1)
                act.wait_ge(u_taken, k + 1)
                for b in range(2):
                    r = slice(k * QT + b * BT, k * QT + (b + 1) * BT)
                    act.activation(pw[:, r, :].rearrange("p t f -> p (t f)"), pP[b][:, :], ACT.Copy)
                    act.activation(tmp[:, r, :].rearrange("p t f -> p (t f)"), pP[b][:, :],
                                   ACT.Square).then_inc(p_squared, 1)

            act.dma_start(waTs, waT).then_inc(w_in, 16)
            act.dma_start(a2[:, :], a).then_inc(w_in, 16)
            act.wait_ge(v_copied, 1)
            act.dma_start(wgeT[1:P, 1:F], wgT).then_inc(w_in, 16)
            act.dma_start(wae[1:P, 1:F], wa[1:P, 1:F]).then_inc(w_in, 16)
            act.wait_ge(rstd_arg, 1)
            act.activation(rstd[:, :], rstd[:, :], ACT.Sqrt).then_inc(rstd_ready, 1)
            relu(0)
            relu(1)
            square(0)
            keep_transposes(0)
            relu(2)
            square(1)
            keep_transposes(1)
            relu(3)
            keep_products(0)
            square(2)
            keep_transposes(2)
            keep_products(1)
            square(3)
            keep_transposes(3)
            act.wait_ge(root_arg, 1)
            act.activation(y[:, :], rr[:, :], ACT.Sqrt).then_inc(root_done, 1)
            keep_products(2)
            act.wait_ge(ln_arg, 1)
            act.activation(lw[:, :], z[:, :], ACT.Ln, bias=1.0).then_inc(ln_done, 1)
            keep_products(3)
            act.wait_ge(root_arg, 2)
            act.activation(nn[:, :], n2[:, :], ACT.Sqrt).then_inc(root_done, 1)
            act.wait_ge(root_done, 2)
            act.activation(ep[:, :], nn[:, :], ACT.Exp)
            act.activation(en[:, :], nn[:, :], ACT.Exp, scale=-1.0).then_inc(exps_done, 1)
            act.wait_ge(root_arg, 3)
            act.activation(y[:, 0:TILES], rr[:, 0:TILES], ACT.Sqrt, scale=2.0 ** -12).then_inc(root_done, 1)
            act.wait_ge(ln_arg, 2)
            act.activation(lw[:, :], w[:, :], ACT.Ln)
            act.activation(lw2[:, :], w2[:, :], ACT.Ln).then_inc(ln_done, 1)
            act.wait_ge(d_ready, 1)
            act.activation(pp[:, :], dd[:, :], ACT.Exp, bias=negD[:, :]).then_inc(p_ready, 1)
            for k in range(QUARTERS):
                q = quarter(k)
                act.wait_ge(g_ready, k + 1)
                act.activation(ghi[:, q, :], pw[:, q, :], ACT.Copy).then_inc(hi_ready, 1)

            def finish(grp, nt, banks, chunks):
                act.wait_ge(masks_used, RING + chunks)
                for n, b in enumerate(banks):
                    cols = slice(n * BANK, (n + 1) * BANK)
                    act.activation(numT[:, cols], acc[b][:, :], ACT.Copy)
                    last = act.activation(zr[:, cols], acc[b][0:1, :], ACT.Relu, bias=1.0, scale=-1e34)
                last.then_inc(num_ready, 1)
                act.wait_ge(mn_ready, grp + 1)
                act.activation(mn[:, 0:nt, :], mn[:, 0:nt, :], ACT.Exp).then_inc(ex_ready, 1)
                act.wait_ge(em_ready, grp + 1)
                for t in range(nt):
                    last = act.activation(junk[t // BT][:, t % BT, 1:F], hp[:, t, 1:F], ACT.Square,
                                          accum_out=s1[:, t:t + 1])
                last.then_inc(s1_ready, 1)
                act.wait_ge(erw_ready, grp + 1)
                act.activation(ey[:, 0:2 * nt], erw[:, 0:2 * nt], ACT.Sqrt)
                act.activation(eth[:, 0:nt], erw[:, 0:nt], ACT.Sqrt, bias=1.0).then_inc(ey_ready, 1)
                act.wait_ge(ez_ready, grp + 1)
                act.activation(elw[:, 0:nt], ez[:, 0:nt], ACT.Ln, bias=1.0).then_inc(elw_ready, 1)
                act.wait_ge(ef_ready, grp + 1)
                for t in range(nt):
                    last = act.activation(hp[:, t, 1:F], hp[:, t, 1:F], ACT.Sigmoid, scale=ef[:, t:t + 1])
                step(last)
                for t in range(nt):
                    last = act.activation(junk[t // BT][:, t % BT, 1:F], hp[:, t, 1:F], ACT.Square,
                                          accum_out=s2[:, t:t + 1])
                step(last)
                step(act.activation(exn[:, 0:nt], s2[:, 0:nt], ACT.Sqrt))
                act.activation(eep[:, 0:nt], exn[:, 0:nt], ACT.Exp)
                act.activation(een[:, 0:nt], exn[:, 0:nt], ACT.Exp, scale=-1.0).then_inc(eexp_ready, 1)

            with act.Fori(0, WIDES) as g:
                step.enter(g, 3)
                finish(g, WIDE, (0, 1), (g + 1) * SLOTS)
                step.leave(WIDES)
            for n in range(NARROWS):
                finish(WIDES + n, NARROW, (n,), CHUNKS - (NARROWS - 1 - n) * (CHUNKS - WIDES * SLOTS) // NARROWS)

        @block.vector
        def _(dve):
            step = Chain(dve, dve_step)

            dve.memset(wge, 0.0)
            dve.memset(wgeT, 0.0)
            step(dve.memset(wae[:, :], 0.0))
            dve.memset(wae[0:1, 0:1], 1.0).then_inc(v_copied, 1)
            dve.memset(zr[:, :], 0.0).then_inc(masks_used, RING)
            dve.memset(rden[:, :], 0.0).then_inc(o_stored, 16)

            for k in range(QUARTERS):
                dve.wait_ge(x_in[k], 16)
                for n in range(QT):
                    last = dve.bn_stats(stats[:, k * QT + n, :], xs[:, k * QT + n, :])
                step(last)
                if k == 1:
                    dve.wait_ge(v_made, 1)
                    dve.tensor_copy(v2[:, :], pV).then_inc(v_copied, 1)
            dve.wait_ge(w_made, 1)
            dve.tensor_copy(wge[:, 0:1], pW[:, 1:2]).then_inc(w_copied, 1)
            dve.tensor_tensor(mean[:, :], stats[:, :, 1], stats[:, :, 4], ALU.add)
            dve.tensor_tensor(t2[:, :], stats[:, :, 2], stats[:, :, 5], ALU.add)
            step(dve.tensor_tensor(t1[:, :], stats[:, :, 1], stats[:, :, 4], ALU.subtract))
            step(dve.tensor_tensor(t1[:, :], t1[:, :], t1[:, :], ALU.mult))
            step(dve.scalar_tensor_tensor(t1[:, :], t1[:, :], F / 4.0, t2[:, :], ALU.mult, ALU.add))
            step(dve.tensor_scalar(var[:, :], t1[:, :], 1.0 / F, 1e-5, ALU.mult, ALU.add))
            dve.reciprocal(rstd[:, :], var[:, :]).then_inc(rstd_arg, 1)
            step(dve.tensor_scalar(mean[:, :], mean[:, :], 0.5, None, ALU.mult))
            dve.wait_ge(rstd_ready, 1)

            def norm(k):
                for n in range(QT):
                    t = k * QT + n
                    last = dve.tensor_scalar(u[:, t, :], xs[:, t, :], mean[:, t:t + 1], rstd[:, t:t + 1],
                                             ALU.subtract, ALU.mult)
                last.then_inc(normed, 1)

            def parts(k):
                q, b = quarter(k), k % 2
                dve.wait_ge(u_ready, k + 1)
                if k >= 2:
                    dve.wait_ge(uT_made, k - 1)
                dve.tensor_copy(nat[:, b, 0, :, :], u[:, q, :]).then_inc(hi_made, 1)
                dve.wait_ge(hi_made, k + 1)
                dve.tensor_tensor(nat[:, b, 1, :, :], u[:, q, :], nat[:, b, 0, :, :],
                                  ALU.subtract).then_inc(nat_ready, 1)

            def u_norm(k):
                dve.wait_ge(u_squared, k + 1)
                dve.tensor_reduce(usum[:, quarter(k)], tmp[:, quarter(k), 1:F], AX.X, ALU.add).then_inc(u_taken, 1)

            def p_norm(k):
                dve.wait_ge(p_squared, 2 * k + 2)
                step(dve.tensor_reduce(psum2[:, quarter(k)], tmp[:, quarter(k), 1:F], AX.X, ALU.add))

            norm(0)
            norm(1)
            parts(0)
            norm(2)
            parts(1)
            norm(3)
            u_norm(0)
            parts(2)
            u_norm(1)
            parts(3)
            u_norm(2)
            step(dve.tensor_scalar(tm[:, :], u[:, :, 0], -1.0, EPS, ALU.add, ALU.max))
            dve.scalar_tensor_tensor(rr[:, 0:TILES], tm[:, :], 2.0, tm[:, :], ALU.add, ALU.mult)
            u_norm(3)
            dve.wait_ge(u_taken, QUARTERS)
            step(dve.tensor_scalar(rr[:, TILES:], usum[:, :], 1e-30, None, ALU.max))
            dve.sem_inc(root_arg, 1)
            p_norm(0)
            dve.wait_ge(root_done, 1)
            step(dve.tensor_tensor(z[:, :], tm[:, :], y[:, 0:TILES], ALU.add))
            dve.sem_inc(ln_arg, 1)
            p_norm(1)
            step(dve.reciprocal(coef[:, :], y[:, TILES:]))

            def log1p_factor(z_, w_):
                step(dve.tensor_scalar(w_, z_, 1.0, -1.0, ALU.add, ALU.add))
                step(dve.reciprocal(w_, w_))
                step(dve.tensor_tensor(w_, z_, w_, ALU.mult))

            log1p_factor(z[:, :], w[:, :])
            step(dve.tensor_tensor(coef[:, :], coef[:, :], w[:, :], ALU.mult))
            dve.wait_ge(ln_done, 1)
            step(dve.tensor_tensor(coef[:, :], coef[:, :], lw[:, :], ALU.mult))
            p_norm(2)
            p_norm(3)
            dve.sem_inc(tmp_free, 1)
            step(dve.tensor_tensor(n2[:, :], coef[:, :], coef[:, :], ALU.mult))
            step(dve.tensor_tensor(n2[:, :], n2[:, :], psum2[:, :], ALU.mult))
            step(dve.tensor_scalar(n2[:, :], n2[:, :], 1e-30, None, ALU.max))
            dve.sem_inc(root_arg, 1)
            step(dve.tensor_scalar(t1[:, :], n2[:, :], 1.0 / 42.0, 1.0, ALU.mult, ALU.add))
            step(dve.scalar_tensor_tensor(t1[:, :], t1[:, :], 1.0 / 20.0, n2[:, :], ALU.mult, ALU.mult))
            step(dve.scalar_tensor_tensor(t1[:, :], t1[:, :], 1.0, n2[:, :], ALU.add, ALU.mult))
            step(dve.tensor_scalar(t1[:, :], t1[:, :], 1.0 / 6.0, 1.0, ALU.mult, ALU.add))
            dve.wait_ge(root_done, 2)
            dve.reciprocal(rn[:, :], nn[:, :])
            step(dve.tensor_tensor(t1[:, :], t1[:, :], nn[:, :], ALU.mult))
            step(dve.scalar_tensor_tensor(t1[:, :], n2[:, :], 0.25, t1[:, :], ALU.is_lt, ALU.mult))
            dve.wait_ge(exps_done, 1)
            step(dve.tensor_tensor(t2[:, :], ep[:, :], en[:, :], ALU.subtract))
            step(dve.tensor_scalar(t2[:, :], t2[:, :], 0.5, None, ALU.mult))
            step(dve.scalar_tensor_tensor(t2[:, :], n2[:, :], 0.25, t2[:, :], ALU.is_ge, ALU.mult))
            step(dve.tensor_tensor(sh[:, :], t1[:, :], t2[:, :], ALU.add))
            step(dve.tensor_scalar(sh[:, :], sh[:, :], ROOT_EPS, None, ALU.max))
            step(dve.tensor_tensor(t1[:, :], sh[:, :], sh[:, :], ALU.mult))
            step(dve.tensor_scalar(rr[:, 0:TILES], t1[:, :], 1.0, None, ALU.add))
            dve.sem_inc(root_arg, 1)
            dve.wait_ge(root_done, 3)
            step(dve.tensor_scalar(t2[:, :], y[:, 0:TILES], 64.0, 1.0, ALU.mult, ALU.add))
            step(dve.reciprocal(t2[:, :], t2[:, :]))
            step(dve.tensor_tensor(t2[:, :], t1[:, :], t2[:, :], ALU.mult))
            step(dve.tensor_tensor(z[:, :], sh[:, :], t2[:, :], ALU.add))
            step(dve.tensor_scalar(t1[:, :], z[:, :], 1.0, None, ALU.add))
            dve.tensor_scalar(w[:, :], t1[:, :], 2.0 ** 60, None, ALU.min)
            step(dve.tensor_scalar(w2[:, :], t1[:, :], 2.0 ** -60, 1.0, ALU.mult, ALU.max))
            dve.sem_inc(ln_arg, 1)
            log1p_factor(z[:, :], t2[:, :])
            step(dve.tensor_tensor(t2[:, :], t2[:, :], coef[:, :], ALU.mult))
            dve.wait_ge(ln_done, 2)
            step(dve.tensor_tensor(lw[:, :], lw[:, :], lw2[:, :], ALU.add))
            step(dve.tensor_tensor(kap[:, :], lw[:, :], t2[:, :], ALU.mult))
            step(dve.tensor_tensor(kap[:, :], kap[:, :], rn[:, :], ALU.mult))
            step(dve.tensor_tensor(dd[:, :], kap[:, :], pw[:, :, 0], ALU.mult))
            dve.tensor_reduce(ext[:, 0:1], dd[:, :], AX.X, ALU.max)
            step(dve.tensor_scalar(t1[:, :], dd[:, :], -1.0, None, ALU.mult))
            dve.tensor_reduce(ext[:, 1:2], t1[:, :], AX.X, ALU.max)
            dve.tensor_reduce(ext[:, 2:3], v2[:, :], AX.X, ALU.max, apply_absolute_value=True).then_inc(ext_ready, 1)
            dve.wait_ge(extT_made, 1)
            step(dve.tensor_reduce(extT[:, :], pE, AX.X, ALU.max))
            dve.tensor_scalar(exd[:, :], idf[0:3, 0:3], extT[:, 0:1], None, ALU.mult).then_inc(exd_ready, 1)
            dve.wait_ge(exb_made, 1)
            dve.tensor_scalar(negD[:, :], pB[:, 0:1], -1.0, None, ALU.mult).then_inc(d_ready, 1)
            dve.tensor_copy(exb[:, :], pB)
            dve.wait_ge(p_ready, 1)
            step(dve.tensor_scalar(pw2[:, :].bitcast(i32), pp[:, :].bitcast(i32), 0x7F800000, None,
                                   ALU.bitwise_and))
            step(dve.tensor_scalar(qq[:, :].bitcast(i32), pp[:, :].bitcast(i32), 0x007FFFFF, 0x3F800000,
                                   ALU.bitwise_and, ALU.bitwise_or))
            step(dve.tensor_scalar(qq[:, :], qq[:, :], G_SCALE, None, ALU.mult))
            step(dve.tensor_tensor(gs[:, :], qq[:, :], kap[:, :], ALU.mult))
            dve.reciprocal(iq[:, :], qq[:, :])
            for k in range(QUARTERS):
                q = quarter(k)
                step(dve.tensor_tensor(pw[:, q, :], pw[:, q, :], gs[:, q].unsqueeze(2).to_broadcast([P, QT, F]),
                                       ALU.mult))
                dve.tensor_copy(pw[:, q, 0], qq[:, q]).then_inc(g_ready, 1)

            def low(k):
                dve.wait_ge(hi_ready, k + 1)
                dve.tensor_tensor(glo[:, quarter(k), :], pw[:, quarter(k), :], ghi[:, quarter(k), :],
                                  ALU.subtract).then_inc(lo_ready, 1)

            def row_sum():
                dve.wait_ge(h_summed, 1)
                dve.tensor_copy(hr[:, :], pH).then_inc(hr_ready, 1)
                dve.wait_ge(hs_made, 1)
                dve.tensor_copy(hs[:, :], pC).then_inc(hs_ready, 1)
                dve.wait_ge(r_made, 1)
                step(dve.tensor_copy(rf[:, :], pR))
                for n in range(3):
                    last = dve.tensor_copy(R[:, n, :], rf[:, :])
                    if n < 2:
                        step(last)
                        step(dve.tensor_tensor(rf[:, :], rf[:, :], R[:, n, :], ALU.subtract))
                last.then_inc(r_ready, 1)

            def masks(turn, s, chunk, nt, tiles):
                dve.wait_ge(adj_in[s], turn * 16 + 16)
                dve.wait_ge(masks_used, turn * SLOTS + s + 1)
                w = nt * P
                for n in range(tiles):
                    cols = slice(n * w, (n + 1) * w)
                    j = chunk * tiles + n
                    last = dve.tensor_scalar(mask[:, s % RING, cols], raw[:, s, cols], 0.0, pw2[:, j:j + 1],
                                             ALU.is_gt, ALU.mult)
                last.then_inc(masks_ready, 1)

            def divide(grp, nt):
                dve.wait_ge(e_ready, grp + 1)
                for n in range(nt // BT):
                    last = dve.reciprocal(rden[:, n * BT:(n + 1) * BT], E[n][:, :, 0])
                step(last)
                dve.wait_ge(o_stored, grp * 16 + 16)
                for n in range(nt // BT):
                    r = slice(n * BT, (n + 1) * BT)
                    last = dve.tensor_tensor(hp[:, r, :], E[n], rden[:, r].unsqueeze(2).to_broadcast([P, BT, F]),
                                             ALU.mult)
                step(last)
                dve.tensor_scalar(mn[:, 0:nt, :], hp[:, 0:nt, :], 0.0, None, ALU.min).then_inc(mn_ready, 1)

            def elu(grp, nt):
                dve.wait_ge(ex_ready, grp + 1)
                dve.scalar_tensor_tensor(hp[:, 0:nt, :], mn[:, 0:nt, :], -1.0, hp[:, 0:nt, :], ALU.add,
                                         ALU.max).then_inc(em_ready, 1)

            def root_args(grp, nt):
                dve.wait_ge(s1_ready, grp + 1)
                step(dve.tensor_scalar(erw[:, 0:nt], s1[:, 0:nt], ROOT_EPS ** 2, None, ALU.max))
                dve.tensor_scalar(erw[:, nt:2 * nt], s1[:, 0:nt], 1e-30, None, ALU.max).then_inc(erw_ready, 1)

            def log_arg(grp, nt):
                dve.wait_ge(ey_ready, grp + 1)
                step(dve.tensor_scalar(etm[:, 0:nt], eth[:, 0:nt], 1.0, None, ALU.add))
                step(dve.reciprocal(etm[:, 0:nt], etm[:, 0:nt]))
                step(dve.tensor_tensor(etm[:, 0:nt], erw[:, 0:nt], etm[:, 0:nt], ALU.mult))
                dve.tensor_tensor(ez[:, 0:nt], ey[:, 0:nt], etm[:, 0:nt], ALU.add).then_inc(ez_ready, 1)

            def log_scale(grp, nt):
                dve.wait_ge(ez_ready, grp + 1)
                log1p_factor(ez[:, 0:nt], ew[:, 0:nt])
                step(dve.reciprocal(etm[:, 0:nt], ey[:, nt:2 * nt]))
                step(dve.tensor_tensor(ew[:, 0:nt], ew[:, 0:nt], etm[:, 0:nt], ALU.mult))
                dve.wait_ge(elw_ready, grp + 1)
                dve.tensor_tensor(ef[:, 0:nt], ew[:, 0:nt], elw[:, 0:nt], ALU.mult).then_inc(ef_ready, 1)

            def output(grp, nt, t0):
                dve.wait_ge(eexp_ready, grp + 1)
                step(dve.tensor_scalar(exn[:, 0:nt], exn[:, 0:nt], 1e-15, None, ALU.max))
                dve.reciprocal(exn[:, 0:nt], exn[:, 0:nt])
                dve.tensor_tensor(ech[:, 0:nt], eep[:, 0:nt], een[:, 0:nt], ALU.add)
                step(dve.tensor_tensor(esh[:, 0:nt], eep[:, 0:nt], een[:, 0:nt], ALU.subtract))
                step(dve.scalar_tensor_tensor(esh[:, 0:nt], esh[:, 0:nt], 0.5, exn[:, 0:nt], ALU.mult, ALU.mult))
                for t in range(nt):
                    dve.scalar_tensor_tensor(hp[:, t, 1:F], hp[:, t, 1:F], esh[:, t:t + 1],
                                             xs[:, t0 + t, 1:F], ALU.mult, ALU.add)
                dve.scalar_tensor_tensor(hp[:, 0:nt, 0], ech[:, 0:nt], 0.5,
                                         xs[:, bass.ds(t0, nt), 0], ALU.mult, ALU.add).then_inc(o_ready, 1)

            def wide(grp):
                for s in range(SLOTS):
                    masks(grp, s, s, WIDE, SLOT // (WIDE * P))
                    if s == 2:
                        divide(grp - 1, WIDE)
                    elif s == 3:
                        elu(grp - 1, WIDE)
                    elif s == 4:
                        root_args(grp - 1, WIDE)
                    elif s == 5:
                        log_arg(grp - 1, WIDE)
                        log_scale(grp - 1, WIDE)
                    elif s == 7:
                        output(grp - 1, WIDE, (grp - 1) * WIDE)

            for s in range(SLOTS):
                if s < half:
                    for k in range(s * QUARTERS // half, (s + 1) * QUARTERS // half):
                        low(k)
                if s == half:
                    dve.wait_ge(lo_ready, QUARTERS)
                    dve.wait_ge(h_summed, 1)
                masks(0, s, s, WIDE, SLOT // (WIDE * P))
                if s == half:
                    row_sum()
            with dve.Fori(1, WIDES) as g:
                step.enter(g - 1, STEPS)
                wide(g)
                step.leave(WIDES - 1)

            chunks = SLOTS // NARROWS
            for n in range(NARROWS):
                g = WIDES + n
                nt, t0 = (WIDE, (WIDES - 1) * WIDE) if n == 0 else (NARROW, (g - 1 - WIDES) * NARROW + WIDES * WIDE)
                for c in range(chunks):
                    masks(WIDES, n * chunks + c, c, NARROW, SLOT // (NARROW * P))
                    if c == 0:
                        divide(g - 1, nt)
                        elu(g - 1, nt)
                    elif c == 1:
                        root_args(g - 1, nt)
                        log_arg(g - 1, nt)
                        log_scale(g - 1, nt)
                    elif c == 2:
                        output(g - 1, nt, t0)
            g = GROUPS - 1
            divide(g, NARROW)
            elu(g, NARROW)
            root_args(g, NARROW)
            log_arg(g, NARROW)
            log_scale(g, NARROW)
            output(g, NARROW, TILES - NARROW)

        @block.tensor
        def _(pe):
            pe.wait_ge(id_ready, 2)
            pe.wait_ge(w_in, 5 * 16)
            pe.matmul(pV, waTs, a2[:, :], start=True, stop=True).then_inc(v_made, 1)
            pe.wait_ge(v_copied, 2)
            pe.matmul(pW, wgeT, v2[:, :], start=True, stop=True).then_inc(w_made, 1)

            def transposes(k):
                pe.wait_ge(nat_ready, k + 1)
                if k >= 2:
                    pe.wait_ge(uT_ready, 2 * (k - 1))
                for part in range(2):
                    to = pT[k % 2 * 2 + part][:, :].bitcast(f16)
                    for n in range(QT):
                        last = pe.transpose(to[:, n * P:(n + 1) * P], nat[:, k % 2, part, n, :], ident)
                last.then_inc(uT_made, 1)

            def products(k):
                pe.wait_ge(uT_ready, 2 * k + 2)
                if k == 0:
                    pe.wait_ge(split, 5)
                else:
                    pe.wait_ge(p_squared, 2 * k)
                for n in range(QT):
                    to = pP[n // BT][:, n % BT * F:(n % BT + 1) * F]
                    for i in range(6):
                        last = pe.matmul(to, uT[:, k % 2, i // 3, n, :], wparts[:, i % 3, :],
                                         start=(i == 0), stop=(i == 5))
                last.then_inc(p_made, 1)

            transposes(0)
            for k in range(1, QUARTERS):
                transposes(k)
                products(k - 1)
            products(QUARTERS - 1)

            pe.wait_ge(ext_ready, 1)
            pe.transpose(pE, ext[:, :], idf).then_inc(extT_made, 1)
            pe.wait_ge(exd_ready, 1)
            pe.matmul(pB, ones[:, :], exd[:, :], start=True, stop=True).then_inc(exb_made, 1)
            for t in range(TILES):
                if t % QT == 0:
                    pe.wait_ge(g_ready, t // QT + 1)
                last = pe.matmul(pH, iq[:, t:t + 1], pw[:, t, :], start=(t == 0), stop=(t == TILES - 1))
            last.then_inc(h_summed, 1)

            def row_sum():
                pe.wait_ge(hr_ready, 1)
                pe.matmul(pC, hr[:, :], ones[0:1, 0:1], start=True, stop=True).then_inc(hs_made, 1)
                pe.wait_ge(hs_ready, 1)
                pe.matmul(pR, hs[:, :], wae[:, :], start=True, stop=True).then_inc(r_made, 1)

            def gather(turn, s, chunk, nt, tiles, banks, first=False):
                pe.wait_ge(masks_ready, turn * SLOTS + s + 1)
                if first:
                    pe.wait_ge(lo_ready, min(s, QUARTERS - 1) + 1)
                for n in range(tiles):
                    j = chunk * tiles + n
                    for part, g in enumerate((ghi, glo)):
                        for i, b in enumerate(banks):
                            at = n * nt * P + i * BANK
                            last = pe.matmul(acc[b][:, :], g[:, j, :], mask[:, s % RING, at:at + BANK],
                                             start=(j == 0 and part == 0), stop=(j == TILES - 1 and part == 1))
                last.then_inc(masks_used, 1)

            def attend(grp, nt):
                pe.wait_ge(num_ready, grp + 1)
                for t in range(nt):
                    e = E[t // BT][:, t % BT, :]
                    rows = slice(t * P, (t + 1) * P)
                    pe.matmul(e, numT[:, rows], wae[:, :], start=True, stop=False)
                    for part in range(3):
                        last = pe.matmul(e, zr[0:1, rows], R[0:1, part, :], start=False, stop=(part == 2))
                last.then_inc(e_ready, 1)

            for s in range(SLOTS):
                gather(0, s, s, WIDE, SLOT // (WIDE * P), (0, 1), first=True)
                if s == half:
                    row_sum()
            pe.wait_ge(r_ready, 1)
            with pe.Fori(1, WIDES) as g:
                attend(g - 1, WIDE)
                for s in range(SLOTS):
                    gather(g, s, s, WIDE, SLOT // (WIDE * P), (0, 1))
            chunks = SLOTS // NARROWS
            for n in range(NARROWS):
                attend(WIDES + n - 1, WIDE if n == 0 else NARROW)
                for c in range(chunks):
                    gather(WIDES, n * chunks + c, c, NARROW, SLOT // (NARROW * P), (n,))
            attend(GROUPS - 1, NARROW)


STEPS = 14


def kernel(**inputs):
    import numpy as np
    import concourse.bacc as bacc
    from concourse.bass_utils import run_bass_kernel_spmd

    f = np.ascontiguousarray
    adj = np.asarray(inputs["adj"]).reshape(P, TILES, P, TILES)
    chunks, done = [], 0
    for nt in [WIDE] * WIDES + [NARROW] * NARROWS:
        tiles = SLOT // (nt * P)
        group = adj[:, done:done + nt].reshape(P, nt, P, TILES // tiles, tiles)
        chunks.append(group.transpose(3, 2, 4, 1, 0).reshape(-1, P, SLOT))
        done += nt
    adj = np.concatenate(chunks)
    wg, wa = np.asarray(inputs["L0_gnn_W_gcn"]), np.asarray(inputs["L0_gnn_W_att"])
    arrays = {
        "x": f(inputs["x"]).reshape(P, TILES, F),
        "adj": f(adj),
        "wg": f(wg), "wgT": f(wg.T), "wa": f(wa), "waT": f(wa.T),
        "a": f(np.asarray(inputs["L0_gnn_a_att"]).reshape(2, F).T),
    }
    nc = bacc.Bacc("TRN2", target_bir_lowering=False, num_devices=1)
    args = [nc.dram_tensor(n, v.shape, mybir.dt.from_np(v.dtype), kind="ExternalInput").ap()
            for n, v in arrays.items()]
    out = nc.dram_tensor("out", (P, TILES * F), mybir.dt.float32, kind="ExternalOutput").ap()
    layer(nc, *args, out)
    r = run_bass_kernel_spmd(nc, [arrays], core_ids=[0])
    return r.results[0]["out"].reshape(N, F)
```

```python
import math

import concourse.bass as bass
from concourse import mybir
from contextlib import ExitStack

P = 128
N = 4096
F = 128
TILES = N // P
SLOT = 4096
SLOTS = 8
RING = 4
WIDE, NARROW = 8, 4
WIDES, NARROWS = 3, 2
GROUPS = WIDES + NARROWS
CHUNKS = TILES * N // SLOT
BANK = 512
QUARTERS = 4
QT = TILES // QUARTERS
EPS = 2.0 ** -23
ROOT_EPS = (EPS * (EPS + 2.0)) ** 0.5
LEAST_LENGTH = math.log(1.0 + EPS + ROOT_EPS)
Q_SCALE = 512.0
SPREAD = 60.0
PENALTY = -1e30


class Chain:

    def __init__(self, eng, sem):
        self.eng, self.sem, self.base, self.n = eng, sem, 0, 0

    def __call__(self, ins):
        self.n += 1
        ins.then_inc(self.sem, 1)
        self.eng.wait_ge(self.sem, self.base + self.n)

    def enter(self, it, per):
        self.before, self.per = self.n, per
        self.base, self.n = it * per + self.before, 0

    def leave(self, trips):
        assert self.n == self.per, self.n
        self.base, self.n = 0, self.before + trips * self.per


def layer(nc, x, adj, wg, wgT, wa, waT, a, out):
    f32, i32, bf16, f16 = mybir.dt.float32, mybir.dt.int32, mybir.dt.bfloat16, mybir.dt.float16
    ALU, ACT, AX = mybir.AluOpType, mybir.ActivationFunctionType, mybir.AxisListType
    ctx = ExitStack()
    with ctx:
        def sb(name, shape, dt=f32):
            return ctx.enter_context(nc.sbuf_tensor("sb_" + name, shape, dt))

        def sem(name):
            return ctx.enter_context(nc.semaphore(name))

        raw = sb("raw", [P, SLOTS, SLOT], i32)
        mask = sb("mask", [P, RING, SLOT], bf16)
        xs = sb("xs", [P, TILES, F])
        G = sb("G", [P, TILES, 2, F], f16)
        ghi, glo = G[:, :, 0, :], G[:, :, 1, :]
        half = RING // 2
        u, pw = (mask[:, h * half:(h + 1) * half, :].rearrange("p a w -> p (a w)").bitcast(f32).rearrange(
            "p (t f) -> p t f", f=F) for h in range(2))
        tmp = raw[:, SLOTS - 1, :].bitcast(f32).rearrange("p (t f) -> p t f", f=F)
        nat, uT = (G[:, h * TILES // 2:(h + 1) * TILES // 2, :, :].rearrange("p t s f -> p (t s) f").rearrange(
            "p (b s t) f -> p b s t f", b=2, s=2) for h in range(2))

        hp = sb("hp", [P, WIDE, F])
        mn = sb("mn", [P, WIDE, F])
        wge, wgeT, waTs, idf = (hp[:, n, :] for n in range(4))
        ident = hp[:, 4, 0:F // 2].bitcast(f16)
        wrest = hp[:, 5, :]
        stats = hp[:, 6:8, :].rearrange("p t f -> p (t f)")[:, 0:6 * TILES].rearrange("p (t s) -> p t s", s=6)
        wparts = sb("wparts", [P, 3, 2, F], bf16)
        w2 = hp[:, 2, :]
        spare = mn[:, :, :].rearrange("p t f -> p (t f)")
        ones = sb("ones", [P, P])
        wae = sb("wae", [P, F])
        a2 = sb("a2", [P, 2])

        def short(n):
            return spare[:, n * TILES:(n + 1) * TILES]

        def col(name, n=TILES, dt=f32):
            return sb(name, [P, n], dt)

        mean, var, usum, psum2, rstd = (short(n) for n in range(5))
        rr = spare[:, 26 * TILES:28 * TILES]
        y = spare[:, 28 * TILES:30 * TILES]
        tm, z, w, lw, n2, coef = (short(n) for n in range(5, 11))
        nn, rn, t1, t2, kap, pp, qq, gs, hmax, spread = (short(n) for n in (*range(16, 24), 24, 25))
        pw2 = col("pw2")
        dd = col("dd")
        iq = col("iq")
        iqp = sb("iqp", [P, TILES, 2], f16)
        ext = col("ext", 3)
        extT = sb("extT", [3, 1])
        exd = sb("exd", [3, 3])
        exb = col("exb", 3)
        unit = col("unit", 1)
        scale, den_scale, mean_scale = col("scale", 1), col("den_scale", 1), col("mean_scale", 1)
        wide_spread = col("wide_spread", 1, i32)
        negD = col("negD", 1)
        hr = sb("hr", [2, 2 * F])
        R = sb("R", [P, F])

        none, rden = col("none", WIDE), col("rden", WIDE)
        s1, s2, erw, ey = col("s1", WIDE), col("s2", WIDE), col("erw", 2 * WIDE), col("ey", 2 * WIDE)
        eth, etm, ez, ew, elw, ef = (col(n, WIDE) for n in ("eth", "etm", "ez", "ew", "elw", "ef"))
        rlen = col("rlen", WIDE)
        exn, eep, een, esh, ech = (col(n, WIDE) for n in ("exn", "eep", "een", "esh", "ech"))

        def left(n):
            flat = raw[:, n, :].bitcast(f32)
            return tuple(flat[:, m * NARROW * F:(m + 1) * NARROW * F].rearrange("p (t f) -> p t f", f=F)
                         for m in range(2))

        def slot(n, dt):
            return raw[:, n, :].bitcast(dt).rearrange("p (t f) -> p t f", f=P)

        edges, logit, feat, scratch = slot(2, i32), slot(3, f32), slot(4, f32), slot(5, f32)
        gid, row_max, diag, zeros = (scratch[:, n, :] for n in range(4))

        bank = [ctx.enter_context(nc.psum_tensor(f"bank{b}", [P, BANK], f32)) for b in range(8)]
        acc = [bk[:, :].rearrange("p (t s f) -> p t s f", s=2, f=F) for bk in bank]
        pT = bank[0:4]
        pP = acc[4:8]
        pV, pW = bank[4][:, 0:2], bank[5][:, 0:F]
        pE, pB = bank[0][0:3, 0:P], bank[1][:, 0:3]
        pMT, pM = bank[0][:, 0:P], bank[1][:, 0:P]
        pH, pR = bank[6][0:2, 0:2 * F], bank[7][:, 0:F]

        adj_in = [sem(f"adj_in{s}") for s in range(SLOTS)]
        x_in = [sem(f"x_in{k}") for k in range(QUARTERS)]
        w_in = sem("w_in")
        zeroed, id_ready = sem("zeroed"), sem("id_ready")
        rstd_arg, rstd_ready, normed, u_ready = sem("rstd_arg"), sem("rstd_ready"), sem("normed"), sem("u_ready")
        hi_made, nat_ready = sem("hi_made"), sem("nat_ready")
        u_squared, u_taken, uT_made, uT_ready = sem("u_squared"), sem("u_taken"), sem("uT_made"), sem("uT_ready")
        v_made, v_copied, w_made, w_copied = sem("v_made"), sem("v_copied"), sem("w_made"), sem("w_copied")
        split = sem("split")
        p_made, p_squared = sem("p_made"), sem("p_squared")
        root_arg, root_done = sem("root_arg"), sem("root_done")
        ln_arg, ln_done = sem("ln_arg"), sem("ln_done")
        ext_ready, extT_made = sem("ext_ready"), sem("extT_made")
        exd_ready, exb_made, d_ready, p_ready = sem("exd_ready"), sem("exb_made"), sem("d_ready"), sem("p_ready")
        h_summed, hr_ready, r_made, r_ready = sem("h_summed"), sem("hr_ready"), sem("r_made"), sem("r_ready")
        g_ready, hi_ready, lo_ready = sem("g_ready"), sem("hi_ready"), sem("lo_ready")
        tmp_free = sem("tmp_free")
        last_masks = sem("last_masks")
        masks_ready, masks_used = sem("masks_ready"), sem("masks_used")
        acc_read, none_ready, fill_ready = sem("acc_read"), sem("none_ready"), sem("fill_ready")
        mn_ready, ex_ready, em_ready, s1_ready = sem("mn_ready"), sem("ex_ready"), sem("em_ready"), sem("s1_ready")
        erw_ready, ey_ready, ez_ready = sem("erw_ready"), sem("ey_ready"), sem("ez_ready")
        elw_ready, ef_ready, eexp_ready, o_ready = sem("elw_ready"), sem("ef_ready"), sem("eexp_ready"), sem("o_ready")
        o_stored = sem("o_stored")
        dve_step, act_step = sem("dve_step"), sem("act_step")
        flag_ready = sem("flag_ready")
        gen_x_in, gen_edges_in, gen_edges_free = sem("gen_x_in"), sem("gen_edges_in"), sem("gen_edges_free")
        gen_id_ready, gen_row_max, gen_maxT_made = sem("gen_id_ready"), sem("gen_row_max"), sem("gen_maxT_made")
        gen_diag_ready, gen_max_made, gen_args = sem("gen_diag_ready"), sem("gen_max_made"), sem("gen_args")
        gen_weights, gen_sums = sem("gen_weights"), sem("gen_sums")

        def quarter(k):
            return slice(k * QT, (k + 1) * QT)

        def general(eng, block_of_tiles, step=None, steps=0):
            per = WIDE // NARROW
            with eng.Fori(0, WIDES) as g:
                if step:
                    step.enter(g, per * steps)
                for b in range(per):
                    block_of_tiles(g * per + b, g * SLOTS, SLOTS, WIDE * P, b * NARROW * P,
                                   g * (per * NARROW * SLOTS) + b * NARROW * SLOTS)
                if step:
                    step.leave(WIDES)
            chunks = SLOTS // NARROWS
            with eng.Fori(0, NARROWS) as n:
                if step:
                    step.enter(n, steps)
                block_of_tiles(n + WIDES * per, n * chunks + WIDES * SLOTS, chunks, NARROW * P, 0,
                               n * (NARROW * chunks) + WIDES * per * NARROW * SLOTS)
                if step:
                    step.leave(NARROWS)

        block = ctx.enter_context(nc.Block())

        @block.sync
        def _(sp):
            for k in range(QUARTERS):
                sp.dma_start(xs[:, quarter(k), :], x[:, quarter(k), :]).then_inc(x_in[k], 16)
                if k == 0:
                    sp.wait_ge(v_copied, 1)
                    sp.dma_start(wge[1:P, 1:F], wg).then_inc(w_in, 16)

            def load(n, s):
                sp.dma_start(raw[:, s, :], adj[n]).then_inc(adj_in[s], 16)

            def store(grp, t0, nt):
                sp.wait_ge(o_ready, grp + 2)
                sp.dma_start(out[:, bass.ds(t0 * F, nt * F)],
                             xs[:, bass.ds(t0, nt), :].rearrange("p t f -> p (t f)")).then_inc(o_stored, 16)

            for s in range(SLOTS):
                if s == SLOTS - 1:
                    sp.wait_ge(tmp_free, 1)
                load(s, s)
            sp.wait_ge(flag_ready, 1)
            far = sp.value_load(wide_spread[0:1, 0:1])
            for s in range(SLOTS):
                sp.wait_ge(masks_ready, s + 1)
                load(SLOTS + s, s)
            with sp.Fori(1, WIDES) as g:
                for s in range(SLOTS):
                    sp.wait_ge(masks_ready, g * SLOTS + s + 1)
                    load(g * SLOTS + SLOTS + s, s)
                store(g - 1, (g - 1) * WIDE, WIDE)
            store(WIDES - 1, (WIDES - 1) * WIDE, WIDE)
            for n in range(NARROWS):
                store(WIDES + n, WIDES * WIDE + n * NARROW, NARROW)
            sp.wait_ge(o_stored, 16 * GROUPS)

            def gen_block(blk, chunk, chunks, width, at, loads):
                for t in range(NARROW):
                    sp.wait_ge(gen_edges_free, blk * NARROW + t + 1)
                    n = SLOT // width
                    for c in range(chunks):
                        src = adj[chunk + c].rearrange("p (n w) -> p n w", w=width)
                        sp.dma_start(edges[:, c * n:(c + 1) * n, :],
                                     src[:, :, at + t * P:at + (t + 1) * P]).then_inc(gen_edges_in, 16)
                store(blk + GROUPS, blk * NARROW, NARROW)

            with sp.If(far > 0):
                for k in range(QUARTERS):
                    sp.dma_start(xs[:, quarter(k), :], x[:, quarter(k), :]).then_inc(gen_x_in, 16)
                general(sp, gen_block)
                sp.wait_ge(o_stored, 16 * (GROUPS + TILES // NARROW))

        @block.gpsimd
        def _(pool):
            pool.memset(idf, 0.0).then_inc(zeroed, 1)
            pool.wait_ge(zeroed, 1)
            pool.affine_select(out=idf, in_=idf, compare_op=ALU.not_equal, fill=1.0, base=0,
                               pattern=[[-1, P]], channel_multiplier=1).then_inc(zeroed, 1)
            pool.memset(ones[:, :], 1.0).then_inc(id_ready, 1)
            pool.wait_ge(zeroed, 2)
            pool.tensor_copy(ident, idf).then_inc(id_ready, 1)

            def three_parts(n, w, at):
                pool.tensor_copy(wparts[:, 0, n, :], w).then_inc(split, 1)
                pool.wait_ge(split, at + 1)
                pool.tensor_tensor(wrest, w, wparts[:, 0, n, :], ALU.subtract).then_inc(split, 1)
                pool.wait_ge(split, at + 2)
                pool.tensor_copy(wparts[:, 1, n, :], wrest).then_inc(split, 1)
                pool.wait_ge(split, at + 3)
                pool.tensor_tensor(wrest, wrest, wparts[:, 1, n, :], ALU.subtract).then_inc(split, 1)
                pool.wait_ge(split, at + 4)
                pool.tensor_copy(wparts[:, 2, n, :], wrest).then_inc(split, 1)
                pool.wait_ge(split, at + 5)

            pool.wait_ge(w_in, 5 * 16)
            three_parts(0, wge, 0)
            pool.wait_ge(w_copied, 1)
            three_parts(1, w2, 5)

            def fill(grp, nt, mn):
                pool.wait_ge(none_ready, grp + 1)
                pool.tensor_tensor(mn[:, 0:nt, :], R[:, :].unsqueeze(1).to_broadcast([P, nt, F]),
                                   none[:, 0:nt].unsqueeze(2).to_broadcast([P, nt, F]),
                                   ALU.mult).then_inc(fill_ready, 1)

            pool.wait_ge(flag_ready, 1)
            far = pool.value_load(wide_spread[0:1, 0:1])
            pool.wait_ge(r_ready, 1)
            with pool.Fori(0, WIDES) as g:
                fill(g, WIDE, mn)
            for n in range(NARROWS):
                fill(WIDES + n, NARROW, left(n)[1])

            def gen_block(blk, *_):
                fill(blk + GROUPS, NARROW, left(0)[1])

            with pool.If(far > 0):
                pool.wait_ge(o_ready, GROUPS + 1)
                pool.memset(gid, 0.0).then_inc(gen_id_ready, 1)
                pool.wait_ge(gen_id_ready, 1)
                pool.affine_select(out=gid, in_=gid, compare_op=ALU.not_equal, fill=1.0, base=0,
                                   pattern=[[-1, P]], channel_multiplier=1).then_inc(gen_id_ready, 1)
                general(pool, gen_block)

        @block.scalar
        def _(act):
            step = Chain(act, act_step)

            def relu(k):
                act.wait_ge(normed, k + 1)
                act.activation(u[:, quarter(k), :], u[:, quarter(k), :], ACT.Relu).then_inc(u_ready, 1)

            def square(k):
                act.wait_ge(u_ready, k + 1)
                act.activation(tmp[:, quarter(k), :], u[:, quarter(k), :], ACT.Square).then_inc(u_squared, 1)

            def keep_transposes(k):
                act.wait_ge(uT_made, k + 1)
                if k >= 2:
                    act.wait_ge(p_made, (k - 1) * QT // 2)
                for part in range(2):
                    act.activation(uT[:, k % 2, part, :, :].rearrange("p t f -> p (t f)"),
                                   pT[k % 2 * 2 + part][:, :].bitcast(f16), ACT.Copy).then_inc(uT_ready, 1)

            def keep_products(k):
                act.wait_ge(u_taken, k + 1)
                for b in range(QT // 2):
                    r = slice(k * QT + b * 2, k * QT + (b + 1) * 2)
                    act.wait_ge(p_made, k * QT // 2 + b + 1)
                    act.activation(pw[:, r, :], pP[b][:, :, 1, :], ACT.Copy)
                    act.activation(tmp[:, r, :], pP[b][:, :, 0, :], ACT.Square).then_inc(p_squared, 1)

            act.dma_start(waTs, waT).then_inc(w_in, 16)
            act.dma_start(a2[:, :], a).then_inc(w_in, 16)
            act.wait_ge(v_copied, 1)
            act.dma_start(wgeT[1:P, 1:F], wgT).then_inc(w_in, 16)
            act.dma_start(wae[:, 1:F], wa[:, 1:F]).then_inc(w_in, 16)
            act.wait_ge(rstd_arg, 1)
            act.activation(rstd[:, :], rstd[:, :], ACT.Sqrt).then_inc(rstd_ready, 1)
            relu(0)
            relu(1)
            square(0)
            keep_transposes(0)
            relu(2)
            square(1)
            keep_transposes(1)
            relu(3)
            keep_products(0)
            square(2)
            keep_transposes(2)
            keep_products(1)
            square(3)
            keep_transposes(3)
            act.wait_ge(root_arg, 1)
            act.activation(y[:, :], rr[:, :], ACT.Sqrt).then_inc(root_done, 1)
            keep_products(2)
            act.wait_ge(ln_arg, 1)
            act.activation(lw[:, :], z[:, :], ACT.Ln, bias=1.0).then_inc(ln_done, 1)
            keep_products(3)
            act.wait_ge(root_arg, 2)
            act.activation(nn[:, :], n2[:, :], ACT.Sqrt).then_inc(root_done, 1)
            act.wait_ge(d_ready, 1)
            act.activation(pp[:, :], dd[:, :], ACT.Exp, bias=negD[:, :]).then_inc(p_ready, 1)
            act.wait_ge(g_ready, 1)
            for t in range(TILES):
                last = act.activation(ghi[:, t, 1:F], pw[:, t, 1:F], ACT.Copy, scale=gs[:, t:t + 1])
                if t % QT == QT - 1:
                    last.then_inc(hi_ready, 1)

            act.wait_ge(flag_ready, 1)
            far = act.value_load(wide_spread[0:1, 0:1])
            act.wait_ge(h_summed, 1)
            act.activation(hr[:, :], pH, ACT.Copy).then_inc(hr_ready, 1)
            act.wait_ge(r_made, 1)
            act.activation(R[:, :], pR, ACT.Copy, scale=mean_scale[:, 0:1]).then_inc(r_ready, 1)

            def finish(grp, nt, hp, mn):
                act.wait_ge(mn_ready, grp + 1)
                act.activation(mn[:, 0:nt, :], mn[:, 0:nt, :], ACT.Exp).then_inc(ex_ready, 1)
                act.wait_ge(em_ready, grp + 1)
                for t in range(nt):
                    last = act.activation(mn[:, t, 1:F], hp[:, t, 1:F], ACT.Square,
                                          accum_out=s1[:, t:t + 1])
                last.then_inc(s1_ready, 1)
                act.wait_ge(erw_ready, grp + 1)
                act.activation(ey[:, 0:2 * nt], erw[:, 0:2 * nt], ACT.Sqrt)
                act.activation(eth[:, 0:nt], erw[:, 0:nt], ACT.Sqrt, bias=1.0).then_inc(ey_ready, 1)
                act.wait_ge(ez_ready, grp + 1)
                act.activation(elw[:, 0:nt], ez[:, 0:nt], ACT.Ln, bias=1.0).then_inc(elw_ready, 1)
                act.wait_ge(ef_ready, grp + 1)
                for t in range(nt):
                    last = act.activation(hp[:, t, 1:F], hp[:, t, 1:F], ACT.Sigmoid, scale=ef[:, t:t + 1])
                step(last)
                for t in range(nt):
                    last = act.activation(mn[:, t, 1:F], hp[:, t, 1:F], ACT.Square,
                                          accum_out=s2[:, t:t + 1])
                step(last)
                step(act.activation(exn[:, 0:nt], s2[:, 0:nt], ACT.Sqrt))
                act.activation(eep[:, 0:nt], exn[:, 0:nt], ACT.Exp)
                act.activation(een[:, 0:nt], exn[:, 0:nt], ACT.Exp, scale=-1.0).then_inc(eexp_ready, 1)

            with act.Fori(0, WIDES) as g:
                step.enter(g, 3)
                finish(g, WIDE, hp, mn)
                step.leave(WIDES)
            for n in range(NARROWS):
                finish(WIDES + n, NARROW, *left(n))

            def gen_block(blk, *_):
                for t in range(NARROW):
                    act.wait_ge(gen_args, blk * NARROW + t + 1)
                    act.activation(logit, logit, ACT.Exp).then_inc(gen_weights, 1)
                finish(blk + GROUPS, NARROW, *left(0))

            with act.If(far > 0):
                general(act, gen_block, step, 3)

        @block.vector
        def _(dve):
            step = Chain(dve, dve_step)

            dve.memset(wge, 0.0)
            dve.memset(wgeT, 0.0).then_inc(v_copied, 1)
            dve.memset(none[:, :], 0.0).then_inc(masks_used, RING)
            dve.memset(rden[:, :], 0.0).then_inc(o_ready, 1)

            for k in range(QUARTERS):
                dve.wait_ge(x_in[k], 16)
                for n in range(QT):
                    last = dve.bn_stats(stats[:, k * QT + n, :], xs[:, k * QT + n, :])
                step(last)
                if k == 1:
                    dve.wait_ge(v_made, 1)
                    dve.tensor_copy(wae[:, 0:1], pV[:, 1:2]).then_inc(v_copied, 1)
            dve.wait_ge(w_made, 1)
            dve.tensor_copy(w2, pW).then_inc(w_copied, 1)
            dve.tensor_tensor(mean[:, :], stats[:, :, 1], stats[:, :, 4], ALU.add)
            dve.tensor_tensor(t2[:, :], stats[:, :, 2], stats[:, :, 5], ALU.add)
            step(dve.tensor_tensor(t1[:, :], stats[:, :, 1], stats[:, :, 4], ALU.subtract))
            step(dve.tensor_tensor(t1[:, :], t1[:, :], t1[:, :], ALU.mult))
            step(dve.scalar_tensor_tensor(t1[:, :], t1[:, :], F / 4.0, t2[:, :], ALU.mult, ALU.add))
            step(dve.tensor_scalar(var[:, :], t1[:, :], 1.0 / F, 1e-5, ALU.mult, ALU.add))
            dve.reciprocal(rstd[:, :], var[:, :]).then_inc(rstd_arg, 1)
            step(dve.tensor_scalar(mean[:, :], mean[:, :], 0.5, None, ALU.mult))
            dve.wait_ge(rstd_ready, 1)

            def norm(k):
                for n in range(QT):
                    t = k * QT + n
                    last = dve.tensor_scalar(u[:, t, :], xs[:, t, :], mean[:, t:t + 1], rstd[:, t:t + 1],
                                             ALU.subtract, ALU.mult)
                last.then_inc(normed, 1)

            def parts(k):
                q, b = quarter(k), k % 2
                dve.wait_ge(u_ready, k + 1)
                if k >= 2:
                    dve.wait_ge(uT_made, k - 1)
                dve.tensor_copy(nat[:, b, 0, :, :], u[:, q, :]).then_inc(hi_made, 1)
                dve.wait_ge(hi_made, k + 1)
                dve.tensor_tensor(nat[:, b, 1, :, :], u[:, q, :], nat[:, b, 0, :, :],
                                  ALU.subtract).then_inc(nat_ready, 1)

            def u_norm(k):
                dve.wait_ge(u_squared, k + 1)
                dve.tensor_reduce(usum[:, quarter(k)], tmp[:, quarter(k), 1:F], AX.X, ALU.add).then_inc(u_taken, 1)

            def p_norm(k):
                dve.wait_ge(p_squared, (k + 1) * QT // 2)
                dve.tensor_reduce(hmax[:, quarter(k)], pw[:, quarter(k), 1:F], AX.X, ALU.max,
                                  apply_absolute_value=True)
                step(dve.tensor_reduce(psum2[:, quarter(k)], tmp[:, quarter(k), 1:F], AX.X, ALU.add))

            norm(0)
            norm(1)
            parts(0)
            norm(2)
            parts(1)
            norm(3)
            u_norm(0)
            parts(2)
            u_norm(1)
            parts(3)
            u_norm(2)
            step(dve.tensor_scalar(tm[:, :], u[:, :, 0], -1.0, EPS, ALU.add, ALU.max))
            dve.scalar_tensor_tensor(rr[:, 0:TILES], tm[:, :], 2.0, tm[:, :], ALU.add, ALU.mult)
            u_norm(3)
            dve.wait_ge(u_taken, QUARTERS)
            step(dve.tensor_scalar(rr[:, TILES:], usum[:, :], 1e-30, None, ALU.max))
            dve.sem_inc(root_arg, 1)
            p_norm(0)
            dve.wait_ge(root_done, 1)
            step(dve.tensor_tensor(z[:, :], tm[:, :], y[:, 0:TILES], ALU.add))
            dve.sem_inc(ln_arg, 1)
            p_norm(1)
            step(dve.reciprocal(coef[:, :], y[:, TILES:]))

            def log1p_factor(z_, w_):
                step(dve.tensor_scalar(w_, z_, 1.0, -1.0, ALU.add, ALU.add))
                step(dve.reciprocal(w_, w_))
                step(dve.tensor_tensor(w_, z_, w_, ALU.mult))

            log1p_factor(z[:, :], w[:, :])
            step(dve.tensor_tensor(coef[:, :], coef[:, :], w[:, :], ALU.mult))
            dve.wait_ge(ln_done, 1)
            step(dve.tensor_tensor(coef[:, :], coef[:, :], lw[:, :], ALU.mult))
            p_norm(2)
            p_norm(3)
            dve.sem_inc(tmp_free, 1)
            step(dve.tensor_tensor(n2[:, :], coef[:, :], coef[:, :], ALU.mult))
            step(dve.tensor_tensor(n2[:, :], n2[:, :], psum2[:, :], ALU.mult))
            step(dve.tensor_scalar(n2[:, :], n2[:, :], 1e-30, None, ALU.max))
            dve.sem_inc(root_arg, 1)
            dve.wait_ge(root_done, 2)
            step(dve.reciprocal(rn[:, :], nn[:, :]))
            step(dve.tensor_scalar(rn[:, :], rn[:, :], LEAST_LENGTH, 1.0, ALU.mult, ALU.max))
            step(dve.tensor_tensor(kap[:, :], rn[:, :], coef[:, :], ALU.mult))
            dve.tensor_tensor(hmax[:, :], hmax[:, :], kap[:, :], ALU.mult)
            step(dve.tensor_tensor(dd[:, :], kap[:, :], pw[:, :, 0], ALU.mult))
            dve.tensor_reduce(ext[:, 0:1], dd[:, :], AX.X, ALU.max)
            step(dve.tensor_scalar(t1[:, :], dd[:, :], -1.0, None, ALU.mult))
            dve.tensor_reduce(ext[:, 2:3], hmax[:, :], AX.X, ALU.max)
            dve.tensor_reduce(ext[:, 1:2], t1[:, :], AX.X, ALU.max).then_inc(ext_ready, 1)
            dve.wait_ge(extT_made, 1)
            step(dve.tensor_reduce(extT[:, :], pE, AX.X, ALU.max))
            dve.tensor_scalar(exd[:, :], idf[0:3, 0:3], extT[:, 0:1], None, ALU.mult).then_inc(exd_ready, 1)
            dve.wait_ge(exb_made, 1)
            dve.tensor_scalar(negD[:, :], pB[:, 0:1], -1.0, None, ALU.mult).then_inc(d_ready, 1)
            step(dve.tensor_copy(exb[:, :], pB))
            dve.tensor_tensor(spread[:, 0:1], exb[:, 0:1], exb[:, 1:2], ALU.add)
            step(dve.tensor_scalar(unit[:, :], exb[:, 2:3], 1e-30, None, ALU.max))
            step(dve.tensor_scalar(unit[:, :].bitcast(i32), unit[:, :].bitcast(i32), 0x7F800000, None,
                                   ALU.bitwise_and))
            dve.tensor_scalar(wide_spread[:, :], spread[:, 0:1], SPREAD, None, ALU.is_gt).then_inc(flag_ready, 1)
            dve.tensor_scalar(mean_scale[:, :], unit[:, :], 2.0 ** -13 / N, None, ALU.mult)
            step(dve.reciprocal(scale[:, :], unit[:, :]))
            dve.tensor_scalar(den_scale[:, :], scale[:, :], 2.0 ** 13 / Q_SCALE, None, ALU.mult)
            step(dve.tensor_scalar(scale[:, :], scale[:, :], 2.0 ** 13, None, ALU.mult))
            dve.wait_ge(p_ready, 1)
            step(dve.tensor_scalar(pw2[:, :].bitcast(i32), pp[:, :].bitcast(i32), 0x7F800000, None,
                                   ALU.bitwise_and))
            step(dve.tensor_scalar(qq[:, :].bitcast(i32), pp[:, :].bitcast(i32), 0x007FFFFF, 0x3F800000,
                                   ALU.bitwise_and, ALU.bitwise_or))
            dve.reciprocal(iq[:, :], qq[:, :])
            dve.scalar_tensor_tensor(gs[:, :], qq[:, :], scale[:, 0:1], kap[:, :], ALU.mult,
                                     ALU.mult).then_inc(g_ready, 1)
            dve.wait_ge(g_ready, 1)
            step(dve.tensor_scalar(qq[:, :], qq[:, :], Q_SCALE, None, ALU.mult))
            def low(k):
                q = quarter(k)
                dve.wait_ge(hi_ready, k + 1)
                for t in range(k * QT, (k + 1) * QT):
                    last = dve.scalar_tensor_tensor(glo[:, t, 1:F], pw[:, t, 1:F], gs[:, t:t + 1], ghi[:, t, 1:F],
                                                    ALU.mult, ALU.subtract)
                step(last)
                step(dve.tensor_copy(ghi[:, q, 0], qq[:, q]))
                dve.tensor_tensor(glo[:, q, 0], qq[:, q], ghi[:, q, 0], ALU.subtract).then_inc(lo_ready, 1)

            def weights_of_sum():
                step(dve.tensor_copy(iqp[:, :, 0], iq[:, :]))
                dve.tensor_tensor(iqp[:, :, 1], iq[:, :], iqp[:, :, 0], ALU.subtract).then_inc(lo_ready, 1)

            def masks(turn, s, chunk, nt, tiles, ready=None):
                dve.wait_ge(adj_in[s], turn * 16 + 16)
                dve.wait_ge(masks_used, turn * SLOTS + s + 1)
                w = nt * P
                for n in range(tiles):
                    cols = slice(n * w, (n + 1) * w)
                    j = chunk * tiles + n
                    last = dve.tensor_scalar(mask[:, s % RING, cols], raw[:, s, cols], 0.0, pw2[:, j:j + 1],
                                             ALU.is_gt, ALU.mult)
                    if ready is not None:
                        last.then_inc(ready, 1)
                if ready is None:
                    last.then_inc(masks_ready, 1)

            def take(grp, nt, banks, chunks, hp, mn, same=True):
                dve.wait_ge(masks_used, RING + chunks)
                if same:
                    dve.wait_ge(o_ready, grp + 1)
                for n, b in enumerate(banks):
                    last = dve.tensor_copy(hp[:, 2 * n:2 * n + 2, :], acc[b][:, :, 0, :])
                step(last)
                for n, b in enumerate(banks):
                    last = dve.tensor_tensor(hp[:, 2 * n:2 * n + 2, :], hp[:, 2 * n:2 * n + 2, :],
                                             acc[b][:, :, 1, :], ALU.add)
                last.then_inc(acc_read, 1)
                dve.wait_ge(acc_read, grp + 1)
                dve.tensor_scalar(none[:, 0:nt], hp[:, 0:nt, 0], 0.0, None, ALU.is_equal).then_inc(none_ready, 1)
                dve.wait_ge(none_ready, grp + 1)
                step(dve.scalar_tensor_tensor(rden[:, 0:nt], hp[:, 0:nt, 0], den_scale[:, 0:1], none[:, 0:nt],
                                              ALU.mult, ALU.add))
                step(dve.reciprocal(rden[:, 0:nt], rden[:, 0:nt]))

            def divide(grp, nt, hp, mn):
                dve.wait_ge(fill_ready, grp + 1)
                for t in range(nt):
                    last = dve.scalar_tensor_tensor(hp[:, t, :], hp[:, t, :], rden[:, t:t + 1], mn[:, t, :],
                                                    ALU.mult, ALU.add)
                step(last)
                dve.tensor_scalar(mn[:, 0:nt, :], hp[:, 0:nt, :], 0.0, None, ALU.min).then_inc(mn_ready, 1)

            def elu(grp, nt, hp, mn):
                dve.wait_ge(ex_ready, grp + 1)
                dve.scalar_tensor_tensor(hp[:, 0:nt, :], mn[:, 0:nt, :], -1.0, hp[:, 0:nt, :], ALU.add,
                                         ALU.max).then_inc(em_ready, 1)

            def root_args(grp, nt):
                dve.wait_ge(s1_ready, grp + 1)
                step(dve.tensor_scalar(erw[:, 0:nt], s1[:, 0:nt], ROOT_EPS ** 2, None, ALU.max))
                dve.tensor_scalar(erw[:, nt:2 * nt], s1[:, 0:nt], 1e-30, None, ALU.max).then_inc(erw_ready, 1)

            def log_arg(grp, nt):
                dve.wait_ge(ey_ready, grp + 1)
                dve.reciprocal(rlen[:, 0:nt], ey[:, nt:2 * nt])
                step(dve.tensor_scalar(etm[:, 0:nt], eth[:, 0:nt], 1.0, None, ALU.add))
                step(dve.reciprocal(etm[:, 0:nt], etm[:, 0:nt]))
                step(dve.tensor_tensor(etm[:, 0:nt], erw[:, 0:nt], etm[:, 0:nt], ALU.mult))
                dve.tensor_tensor(ez[:, 0:nt], ey[:, 0:nt], etm[:, 0:nt], ALU.add).then_inc(ez_ready, 1)

            def log_scale(grp, nt):
                dve.wait_ge(ez_ready, grp + 1)
                log1p_factor(ez[:, 0:nt], ew[:, 0:nt])
                step(dve.tensor_tensor(ew[:, 0:nt], ew[:, 0:nt], rlen[:, 0:nt], ALU.mult))
                dve.wait_ge(elw_ready, grp + 1)
                dve.tensor_tensor(ef[:, 0:nt], ew[:, 0:nt], elw[:, 0:nt], ALU.mult).then_inc(ef_ready, 1)

            def output(grp, nt, t0, hp):
                dve.wait_ge(eexp_ready, grp + 1)
                step(dve.tensor_scalar(exn[:, 0:nt], exn[:, 0:nt], 1e-15, None, ALU.max))
                dve.reciprocal(exn[:, 0:nt], exn[:, 0:nt])
                dve.tensor_tensor(ech[:, 0:nt], eep[:, 0:nt], een[:, 0:nt], ALU.add)
                step(dve.tensor_tensor(esh[:, 0:nt], eep[:, 0:nt], een[:, 0:nt], ALU.subtract))
                step(dve.scalar_tensor_tensor(esh[:, 0:nt], esh[:, 0:nt], 0.5, exn[:, 0:nt], ALU.mult, ALU.mult))
                for t in range(nt):
                    dve.scalar_tensor_tensor(xs[:, t0 + t, 1:F], hp[:, t, 1:F], esh[:, t:t + 1],
                                             xs[:, t0 + t, 1:F], ALU.mult, ALU.add)
                dve.scalar_tensor_tensor(xs[:, bass.ds(t0, nt), 0], ech[:, 0:nt], 0.5,
                                         xs[:, bass.ds(t0, nt), 0], ALU.mult, ALU.add).then_inc(o_ready, 1)

            def wide(grp):
                for s in range(SLOTS):
                    masks(grp, s, s, WIDE, SLOT // (WIDE * P))
                    if s == 1:
                        take(grp - 1, WIDE, range(4), grp * SLOTS, hp, mn)
                    elif s == 2:
                        divide(grp - 1, WIDE, hp, mn)
                    elif s == 3:
                        elu(grp - 1, WIDE, hp, mn)
                    elif s == 4:
                        root_args(grp - 1, WIDE)
                        log_arg(grp - 1, WIDE)
                        log_scale(grp - 1, WIDE)
                    elif s == 7:
                        output(grp - 1, WIDE, (grp - 1) * WIDE, hp)

            for s in range(SLOTS):
                if s == half + 1:
                    weights_of_sum()
                if s >= half:
                    dve.wait_ge(lo_ready, min(2 * (s - half + 1), QUARTERS))
                masks(0, s, s, WIDE, SLOT // (WIDE * P))
                if s < half:
                    low(s)
                elif s == half:
                    low(half)
                    low(half + 1)
            far = dve.value_load(wide_spread[0:1, 0:1])
            with dve.Fori(1, WIDES) as g:
                step.enter(g - 1, STEPS)
                wide(g)
                step.leave(WIDES - 1)

            def narrow(c):
                masks(WIDES, c, c % chunks, NARROW, SLOT // (NARROW * P), last_masks if c == SLOTS - 1 else None)

            chunks = SLOTS // NARROWS
            gw, n0, n1 = WIDES - 1, WIDES, WIDES + 1
            (hp0, mn0), (hp1, mn1) = left(0), left(1)
            narrow(0)
            take(gw, WIDE, range(4), WIDES * SLOTS, hp, mn)
            narrow(1)
            divide(gw, WIDE, hp, mn)
            narrow(2)
            elu(gw, WIDE, hp, mn)
            narrow(3)
            root_args(gw, WIDE)
            log_arg(gw, WIDE)
            log_scale(gw, WIDE)
            narrow(4)
            take(n0, NARROW, (4, 5), WIDES * SLOTS + chunks, hp0, mn0, same=False)
            divide(n0, NARROW, hp0, mn0)
            narrow(5)
            output(gw, WIDE, gw * WIDE, hp)
            elu(n0, NARROW, hp0, mn0)
            narrow(6)
            root_args(n0, NARROW)
            log_arg(n0, NARROW)
            log_scale(n0, NARROW)
            narrow(7)
            take(n1, NARROW, (6, 7), CHUNKS, hp1, mn1, same=False)
            divide(n1, NARROW, hp1, mn1)
            output(n0, NARROW, WIDES * WIDE, hp0)
            elu(n1, NARROW, hp1, mn1)
            root_args(n1, NARROW)
            log_arg(n1, NARROW)
            log_scale(n1, NARROW)
            output(n1, NARROW, WIDES * WIDE + NARROW, hp1)

            def gen_block(blk, chunk, chunks, width, at, loads):
                for t in range(NARROW):
                    dve.wait_ge(gen_edges_in, (loads + (t + 1) * chunks) * 16)
                    step(dve.tensor_scalar(logit, edges, 0.0, PENALTY, ALU.is_le, ALU.mult))
                    dve.tensor_tensor(logit, logit, dd[:, :].unsqueeze(2).to_broadcast([P, TILES, P]),
                                      ALU.add).then_inc(gen_edges_free, 1)
                    dve.wait_ge(gen_edges_free, blk * NARROW + t + 2)
                    dve.tensor_reduce(row_max, logit.rearrange("p t i -> p i t"), AX.X,
                                      ALU.max).then_inc(gen_row_max, 1)
                    dve.wait_ge(gen_maxT_made, blk * NARROW + t + 1)
                    step(dve.tensor_reduce(negD[:, :], pMT, AX.X, ALU.max))
                    step(dve.tensor_scalar(negD[:, :], negD[:, :], PENALTY / 1e10, None, ALU.max))
                    dve.tensor_scalar(diag, gid, negD[:, 0:1], None, ALU.mult).then_inc(gen_diag_ready, 1)
                    dve.wait_ge(gen_max_made, blk * NARROW + t + 1)
                    dve.tensor_tensor(logit, logit, pM.unsqueeze(1).to_broadcast([P, TILES, P]),
                                      ALU.subtract).then_inc(gen_args, 1)
                    dve.wait_ge(gen_sums, blk * NARROW + t + 1)
                grp = blk + GROUPS
                take(grp, NARROW, (4, 5), CHUNKS, hp0, mn0)
                divide(grp, NARROW, hp0, mn0)
                elu(grp, NARROW, hp0, mn0)
                root_args(grp, NARROW)
                log_arg(grp, NARROW)
                log_scale(grp, NARROW)
                output(grp, NARROW, blk * NARROW, hp0)

            with dve.If(far > 0):
                dve.wait_ge(o_ready, GROUPS + 1)
                dve.memset(zeros, 0.0)
                step(dve.tensor_tensor(feat, ghi, glo, ALU.add))
                step(dve.tensor_tensor(feat, feat, iq[:, :].unsqueeze(2).to_broadcast([P, TILES, F]), ALU.mult))
                dve.wait_ge(gen_x_in, QUARTERS * 16)
                dve.wait_ge(gen_id_ready, 2)
                dve.sem_inc(gen_edges_free, 1)
                general(dve, gen_block, step, STEPS + 3 * NARROW)

        @block.tensor
        def _(pe):
            pe.wait_ge(id_ready, 2)
            pe.wait_ge(w_in, 5 * 16)
            pe.matmul(pV, waTs, a2[:, :], start=True, stop=True).then_inc(v_made, 1)
            pe.wait_ge(v_copied, 2)
            pe.matmul(pW, wgeT, wae[:, :], start=True, stop=True).then_inc(w_made, 1)

            def transposes(k):
                pe.wait_ge(nat_ready, k + 1)
                if k >= 2:
                    pe.wait_ge(uT_ready, 2 * (k - 1))
                for part in range(2):
                    to = pT[k % 2 * 2 + part][:, :].bitcast(f16)
                    for n in range(QT):
                        last = pe.transpose(to[:, n * P:(n + 1) * P], nat[:, k % 2, part, n, :], ident)
                last.then_inc(uT_made, 1)

            def products(k):
                pe.wait_ge(uT_ready, 2 * k + 2)
                for n in range(QT):
                    if k == 0 and n == 0:
                        pe.wait_ge(split, 10)
                    elif k > 0 and n % 2 == 0:
                        pe.wait_ge(p_squared, (k - 1) * QT // 2 + n // 2 + 1)
                    to = pP[n // 2][:, n % 2, :, :].rearrange("p s f -> p (s f)")
                    for i in range(5):
                        last = pe.matmul(to, uT[:, k % 2, i // 3, n, :],
                                         wparts[:, i % 3, :, :].rearrange("p s f -> p (s f)"),
                                         start=(i == 0), stop=(i == 4))
                    if n % 2 == 1:
                        last.then_inc(p_made, 1)

            transposes(0)
            for k in range(1, QUARTERS):
                transposes(k)
                products(k - 1)
            products(QUARTERS - 1)

            pe.wait_ge(ext_ready, 1)
            pe.transpose(pE, ext[:, :], idf).then_inc(extT_made, 1)
            pe.wait_ge(exd_ready, 1)
            pe.matmul(pB, ones[0:3, :], exd[:, :], start=True, stop=True).then_inc(exb_made, 1)

            def row_sum():
                pe.wait_ge(lo_ready, QUARTERS + 1)
                for t in range(TILES):
                    last = pe.matmul(pH, iqp[:, t, :], G[:, t, :, :].rearrange("p s f -> p (s f)"),
                                     start=(t == 0), stop=(t == TILES - 1))
                last.then_inc(h_summed, 1)
                pe.wait_ge(hr_ready, 1)
                for part in range(2):
                    last = pe.matmul(pR, ones[0:2, :], hr[:, part * F:(part + 1) * F], start=(part == 0),
                                     stop=(part == 1))
                last.then_inc(r_made, 1)

            def gather(turn, s, chunk, nt, tiles, banks, first=False, ready=None):
                if ready is None:
                    pe.wait_ge(masks_ready, turn * SLOTS + s + 1)
                if first:
                    pe.wait_ge(lo_ready, min(s, QUARTERS - 1) + 1)
                for n in range(tiles):
                    j = chunk * tiles + n
                    if ready is not None:
                        pe.wait_ge(ready, n + 1)
                    for t in range(nt):
                        at = (n * nt + t) * P
                        last = pe.matmul(acc[banks[t // 2]][:, t % 2, :, :].rearrange("p s f -> p (s f)"),
                                         mask[:, s % RING, at:at + P], G[:, j, :, :].rearrange("p s f -> p (s f)"),
                                         start=(j == 0 and t % 2 == 0), stop=(j == TILES - 1 and t % 2 == 1))
                last.then_inc(masks_used, 1)

            for s in range(SLOTS):
                gather(0, s, s, WIDE, SLOT // (WIDE * P), range(4), first=True)
            pe.wait_ge(flag_ready, 1)
            far = pe.value_load(wide_spread[0:1, 0:1])
            row_sum()
            with pe.Fori(1, WIDES) as g:
                pe.wait_ge(acc_read, g)
                for s in range(SLOTS):
                    gather(g, s, s, WIDE, SLOT // (WIDE * P), range(4))
            chunks = SLOTS // NARROWS
            for n in range(NARROWS):
                for c in range(chunks):
                    gather(WIDES, n * chunks + c, c, NARROW, SLOT // (NARROW * P), (4 + 2 * n, 5 + 2 * n),
                           ready=last_masks if n * chunks + c == SLOTS - 1 else None)

            def gen_block(blk, *_):
                pe.wait_ge(acc_read, blk + GROUPS)
                for t in range(NARROW):
                    k = blk * NARROW + t + 1
                    pe.wait_ge(gen_row_max, k)
                    pe.transpose(pMT, row_max, gid).then_inc(gen_maxT_made, 1)
                    pe.wait_ge(gen_diag_ready, k)
                    pe.matmul(pM, ones[:, :], diag, start=True, stop=True).then_inc(gen_max_made, 1)
                    pe.wait_ge(gen_weights, k)
                    to = acc[4 + t // 2]
                    for j in range(TILES):
                        pe.matmul(to[:, t % 2, 0, :], logit[:, j, :], feat[:, j, :],
                                  start=(j == 0 and t % 2 == 0), stop=False)
                    pe.matmul(to[:, t % 2, 1, :], zeros, feat[:, 0, :], start=False,
                              stop=(t % 2 == 1)).then_inc(gen_sums, 1)

            with pe.If(far > 0):
                general(pe, gen_block)


STEPS = 15


def kernel(**inputs):
    import numpy as np
    import concourse.bacc as bacc
    from concourse.bass_utils import run_bass_kernel_spmd

    f = np.ascontiguousarray
    adj = np.asarray(inputs["adj"]).reshape(P, TILES, P, TILES)
    chunks, done = [], 0
    for nt in [WIDE] * WIDES + [NARROW] * NARROWS:
        tiles = SLOT // (nt * P)
        group = adj[:, done:done + nt].reshape(P, nt, P, TILES // tiles, tiles)
        chunks.append(group.transpose(3, 2, 4, 1, 0).reshape(-1, P, SLOT))
        done += nt
    adj = np.concatenate(chunks)
    wg, wa = np.asarray(inputs["L0_gnn_W_gcn"]), np.asarray(inputs["L0_gnn_W_att"])
    arrays = {
        "x": f(inputs["x"]).reshape(P, TILES, F),
        "adj": f(adj),
        "wg": f(wg), "wgT": f(wg.T), "wa": f(wa), "waT": f(wa.T),
        "a": f(np.asarray(inputs["L0_gnn_a_att"]).reshape(2, F).T),
    }
    nc = bacc.Bacc("TRN2", target_bir_lowering=False, num_devices=1)
    args = [nc.dram_tensor(n, v.shape, mybir.dt.from_np(v.dtype), kind="ExternalInput").ap()
            for n, v in arrays.items()]
    out = nc.dram_tensor("out", (P, TILES * F), mybir.dt.float32, kind="ExternalOutput").ap()
    layer(nc, *args, out)
    r = run_bass_kernel_spmd(nc, [arrays], core_ids=[0])
    return r.results[0]["out"].reshape(N, F)
```
